# Optimizing a Trainium2 kernel written in Bass

```python
import numpy as np
import jax
import jax.numpy as jnp

def _softmax(x, axis=-1):
    return jax.nn.softmax(x, axis=axis)

def _gelu(x):
    return jax.nn.gelu(x, approximate=True)

def _silu(x):
    return jax.nn.silu(x)

def _sigmoid(x):
    return jax.nn.sigmoid(x)

def _layernorm(x, axis=-1, eps=1e-05):
    m = jnp.mean(x, axis=axis, keepdims=True)
    v = jnp.var(x, axis=axis, keepdims=True)
    return (x - m) / jnp.sqrt(v + eps)

def _scatter_add(tgt, idx, src, axis=0):
    return tgt.at[idx].add(src)

def _segment_sum(src, seg, n):
    return jax.ops.segment_sum(src, seg, n)
kernel_name = 'mk_adj_ffn_d1_adj_r2_1af256'

def setup_inputs(seed: int=0):
    np.random.seed(seed)
    _w = jnp.asarray

    def _rec_inputs():
        import jax
        import jax.numpy as jnp
        _gk = jax.random.key(seed)
        x = -0.000929 + 1 * jax.random.normal(jax.random.fold_in(_gk, 1), (8192, 128), jnp.float32)
        _w = (1.0 + jnp.arange(8192, dtype=jnp.float32)) ** (-0.5)
        _w = _w / _w.mean()
        _pij = jnp.clip(0.00195312 * _w[:, None] * _w[None, :], 0.0, 1.0)
        _a = jax.random.uniform(jax.random.fold_in(_gk, 2), (8192, 8192)) < _pij
        _a = jnp.logical_or(_a, jnp.eye(8192, dtype=bool))
        _af = _a.astype(jnp.float32)
        _af = _af / jnp.maximum(_af.sum(-1, keepdims=True), 1.0)
        adj = _af
        return (x, adj)
    x, adj = _rec_inputs()

    def _L0_gnn_setup():
        import jax, jax.numpy as jnp
        import numpy as np
        from jax import lax
        D_MODEL = 128
        D_STATE = 16
        D_CONV = 4
        EXPAND = 2
        D_INNER = EXPAND * D_MODEL
        DT_RANK = (D_MODEL + 15) // 16
        N = 2048
        EPS = 1e-05

        def _mamba(h, w_in, conv_w, conv_b, w_xp, w_dt, b_dt, A_log, D_skip, w_out):
            L = h.shape[0]
            xz = h @ w_in
            xc, z = (xz[:, :D_INNER], xz[:, D_INNER:])
            xpad = jnp.pad(xc, ((D_CONV - 1, 0), (0, 0)))
            xconv = sum((xpad[k:k + L] * conv_w[:, k] for k in range(D_CONV))) + conv_b
            u = jax.nn.silu(xconv)
            dbc = u @ w_xp
            dt = jax.nn.softplus(dbc[:, :DT_RANK] @ w_dt + b_dt)
            B = dbc[:, DT_RANK:DT_RANK + D_STATE]
            C = dbc[:, DT_RANK + D_STATE:]
            A = -jnp.exp(A_log)
            dA = jnp.exp(dt[:, :, None] * A[None])
            dBu = dt[:, :, None] * B[:, None, :] * u[:, :, None]

            def step(hst, inp):
                dAt, dBut, Ct = inp
                hst = dAt * hst + dBut
                return (hst, hst @ Ct)
            _, ys = lax.scan(step, jnp.zeros((D_INNER, D_STATE), h.dtype), (dA, dBu, C))
            y = ys + u * D_skip
            y = y * jax.nn.silu(z)
            return y @ w_out
        key = jax.random.key(seed)
        ks = jax.random.split(key, 16)
        x = jax.random.normal(ks[0], (N, D_MODEL), dtype=jnp.float32)
        a = jax.random.uniform(ks[1], (N, N), dtype=jnp.float32)
        adj = a / a.sum(axis=1, keepdims=True)
        s = lambda fi, fo: 1.0 / np.sqrt(fi)
        gcn_w = jax.random.uniform(ks[2], (D_MODEL, D_MODEL), jnp.float32, -s(D_MODEL, 0), s(D_MODEL, 0))
        gcn_b = jnp.zeros((D_MODEL,), jnp.float32)
        ln_g = jnp.ones((D_MODEL,), jnp.float32)
        ln_b = jnp.zeros((D_MODEL,), jnp.float32)
        w_in = jax.random.normal(ks[3], (D_MODEL, 2 * D_INNER), jnp.float32) * s(D_MODEL, 0)
        conv_w = jax.random.normal(ks[4], (D_INNER, D_CONV), jnp.float32) * s(D_CONV, 0)
        conv_b = jnp.zeros((D_INNER,), jnp.float32)
        w_xp = jax.random.normal(ks[5], (D_INNER, DT_RANK + 2 * D_STATE), jnp.float32) * s(D_INNER, 0)
        w_dt = jax.random.normal(ks[6], (DT_RANK, D_INNER), jnp.float32) * s(DT_RANK, 0)
        b_dt = jnp.log(jnp.expm1(jnp.exp(jax.random.uniform(ks[7], (D_INNER,), jnp.float32, np.log(0.001), np.log(0.1)))))
        A_log = jnp.log(jnp.broadcast_to(jnp.arange(1, D_STATE + 1, dtype=jnp.float32), (D_INNER, D_STATE)))
        D_skip = jnp.ones((D_INNER,), jnp.float32)
        w_out = jax.random.normal(ks[8], (D_INNER, D_MODEL), jnp.float32) * s(D_INNER, 0)
        return dict(x=x, adj=adj, gcn_w=gcn_w, gcn_b=gcn_b, ln_g=ln_g, ln_b=ln_b, w_in=w_in, conv_w=conv_w, conv_b=conv_b, w_xp=w_xp, w_dt=w_dt, b_dt=b_dt, A_log=A_log, D_skip=D_skip, w_out=w_out)
    _L0_gnn_all = _L0_gnn_setup()
    _L0_gnn_in = {k: v for k, v in _L0_gnn_all.items() if k in ('gcn_w', 'gcn_b', 'ln_g', 'ln_b', 'w_in', 'conv_w', 'conv_b', 'w_xp', 'w_dt', 'b_dt', 'A_log', 'D_skip', 'w_out')}
    del _L0_gnn_all

    def _L0_ffn_setup():
        import jax, jax.numpy as jnp
        import numpy as np
        C = 128
        HID = 512
        E = 8
        TEMP = 1.0
        key = jax.random.key(seed)
        ks = jax.random.split(key, 7)
        x = jax.random.normal(ks[0], (8, 8192, C), dtype=jnp.float32)
        W1 = jax.random.normal(ks[1], (C, HID), dtype=jnp.float32) * 0.02
        b1 = jnp.zeros((HID,), dtype=jnp.float32)
        Wg = jax.random.normal(ks[2], (HID, E), dtype=jnp.float32) * 0.02
        bg = jnp.zeros((E,), dtype=jnp.float32)
        Wd = jax.random.normal(ks[3], (E, HID, C), dtype=jnp.float32) * 0.02
        bd = jnp.zeros((E, C), dtype=jnp.float32)
        return {'x': x, 'W1': W1, 'b1': b1, 'Wg': Wg, 'bg': bg, 'Wd': Wd, 'bd': bd}
    _L0_ffn_all = _L0_ffn_setup()
    _L0_ffn_in = {k: v for k, v in _L0_ffn_all.items() if k in ('W1', 'b1', 'Wg', 'bg', 'Wd', 'bd')}
    del _L0_ffn_all
    return {'x': x, 'adj': adj, 'L0_gnn_gcn_w': _L0_gnn_in['gcn_w'], 'L0_gnn_gcn_b': _L0_gnn_in['gcn_b'], 'L0_gnn_ln_g': _L0_gnn_in['ln_g'], 'L0_gnn_ln_b': _L0_gnn_in['ln_b'], 'L0_gnn_w_in': _L0_gnn_in['w_in'], 'L0_gnn_conv_w': _L0_gnn_in['conv_w'], 'L0_gnn_conv_b': _L0_gnn_in['conv_b'], 'L0_gnn_w_xp': _L0_gnn_in['w_xp'], 'L0_gnn_w_dt': _L0_gnn_in['w_dt'], 'L0_gnn_b_dt': _L0_gnn_in['b_dt'], 'L0_gnn_A_log': _L0_gnn_in['A_log'], 'L0_gnn_D_skip': _L0_gnn_in['D_skip'], 'L0_gnn_w_out': _L0_gnn_in['w_out'], 'L0_ffn_W1': _L0_ffn_in['W1'], 'L0_ffn_b1': _L0_ffn_in['b1'], 'L0_ffn_Wg': _L0_ffn_in['Wg'], 'L0_ffn_bg': _L0_ffn_in['bg'], 'L0_ffn_Wd': _L0_ffn_in['Wd'], 'L0_ffn_bd': _L0_ffn_in['bd']}

def reference(x, adj, L0_gnn_gcn_w, L0_gnn_gcn_b, L0_gnn_ln_g, L0_gnn_ln_b, L0_gnn_w_in, L0_gnn_conv_w, L0_gnn_conv_b, L0_gnn_w_xp, L0_gnn_w_dt, L0_gnn_b_dt, L0_gnn_A_log, L0_gnn_D_skip, L0_gnn_w_out, L0_ffn_W1, L0_ffn_b1, L0_ffn_Wg, L0_ffn_bg, L0_ffn_Wd, L0_ffn_bd):
    import jax
    import jax.numpy as jnp

    def _L0_gnn_ref(x, adj, gcn_w, gcn_b, ln_g, ln_b, w_in, conv_w, conv_b, w_xp, w_dt, b_dt, A_log, D_skip, w_out):
        import jax, jax.numpy as jnp
        import numpy as np
        from jax import lax
        D_MODEL = 128
        D_STATE = 16
        D_CONV = 4
        EXPAND = 2
        D_INNER = EXPAND * D_MODEL
        DT_RANK = (D_MODEL + 15) // 16
        N = 2048
        EPS = 1e-05

        def _mamba(h, w_in, conv_w, conv_b, w_xp, w_dt, b_dt, A_log, D_skip, w_out):
            L = h.shape[0]
            xz = h @ w_in
            xc, z = (xz[:, :D_INNER], xz[:, D_INNER:])
            xpad = jnp.pad(xc, ((D_CONV - 1, 0), (0, 0)))
            xconv = sum((xpad[k:k + L] * conv_w[:, k] for k in range(D_CONV))) + conv_b
            u = jax.nn.silu(xconv)
            dbc = u @ w_xp
            dt = jax.nn.softplus(dbc[:, :DT_RANK] @ w_dt + b_dt)
            B = dbc[:, DT_RANK:DT_RANK + D_STATE]
            C = dbc[:, DT_RANK + D_STATE:]
            A = -jnp.exp(A_log)
            dA = jnp.exp(dt[:, :, None] * A[None])
            dBu = dt[:, :, None] * B[:, None, :] * u[:, :, None]

            def step(hst, inp):
                dAt, dBut, Ct = inp
                hst = dAt * hst + dBut
                return (hst, hst @ Ct)
            _, ys = lax.scan(step, jnp.zeros((D_INNER, D_STATE), h.dtype), (dA, dBu, C))
            y = ys + u * D_skip
            y = y * jax.nn.silu(z)
            return y @ w_out
        h = jax.nn.relu(adj @ x @ gcn_w + gcn_b)
        mu = h.mean(-1, keepdims=True)
        var = h.var(-1, keepdims=True)
        h = (h - mu) * lax.rsqrt(var + EPS) * ln_g + ln_b
        return _mamba(h, w_in, conv_w, conv_b, w_xp, w_dt, b_dt, A_log, D_skip, w_out)

    def _L0_ffn_ref(x, W1, b1, Wg, bg, Wd, bd):
        import jax, jax.numpy as jnp
        import numpy as np
        C = 128
        HID = 512
        E = 8
        TEMP = 1.0
        orig_shape = x.shape
        xf = x.reshape(-1, orig_shape[-1])
        H = jax.nn.gelu(xf @ W1 + b1, approximate=False)
        probs = jax.nn.softmax((H @ Wg + bg) / TEMP, axis=-1)
        assign = jnp.argmax(probs, axis=-1)
        out = jnp.zeros_like(xf)
        for e in range(Wd.shape[0]):
            y = H @ Wd[e] + bd[e]
            sel = (assign == e)[:, None]
            out = out + jnp.where(sel, probs[:, e:e + 1] * y, 0.0)
        return out.reshape(orig_shape)
    x = x + _L0_gnn_ref(_layernorm(x, axis=-1), adj, L0_gnn_gcn_w, L0_gnn_gcn_b, L0_gnn_ln_g, L0_gnn_ln_b, L0_gnn_w_in, L0_gnn_conv_w, L0_gnn_conv_b, L0_gnn_w_xp, L0_gnn_w_dt, L0_gnn_b_dt, L0_gnn_A_log, L0_gnn_D_skip, L0_gnn_w_out)
    x = x + _L0_ffn_ref(_layernorm(x, axis=-1)[None], L0_ffn_W1, L0_ffn_b1, L0_ffn_Wg, L0_ffn_bg, L0_ffn_Wd, L0_ffn_bd)[0]
    return x

_drawn_inputs = setup_inputs


def setup_inputs(seed=0):
    import zlib

    import numpy as np

    out = dict(_drawn_inputs(seed))
    spreads = {'L0_gnn_gcn_b': (0.0, 0.1),
     'L0_gnn_ln_g': (1.0, 0.2),
     'L0_gnn_ln_b': (0.0, 0.1),
     'L0_gnn_conv_b': (0.0, 0.1),
     'L0_gnn_D_skip': (1.0, 0.2),
     'L0_ffn_b1': (0.0, 0.8),
     'L0_ffn_bg': (0.0, 0.461),
     'L0_ffn_bd': (0.0, 0.626)}
    factors = {'L0_ffn_W1': 5.371, 'L0_ffn_Wg': 5.303, 'L0_ffn_Wd': 7.124}
    for name, (base, spread) in spreads.items():
        noise = np.random.default_rng([zlib.crc32(name.encode()), seed]).standard_normal(out[name].shape)
        drawn = base * np.exp(spread * noise) if base else spread * noise
        out[name] = jnp.asarray(drawn.astype(out[name].dtype))
    for name, factor in factors.items():
        out[name] = (out[name] * factor).astype(out[name].dtype)
    return out
```

```python
from contextlib import ExitStack

import concourse.bass as bass
from concourse import mybir

P = 128
T = 512
SLOTS = 16
GROUP = 4
RING = 4
EPS = 1e-5
CLAMP = 40.0
TAPS = 4
EXPERTS = 8

ALU = mybir.AluOpType
ACT = mybir.ActivationFunctionType
F32 = mybir.dt.float32
BF16 = mybir.dt.bfloat16
AX = mybir.AxisListType.X
EXP_LN_SET = "natural_log_exp_and_others"

COLS = {}
_at = 0
for _name, _n in (("gcn_b", 1), ("ln_g", 1), ("ln_b", 1), ("conv_w", 2 * TAPS), ("conv_b", 2), ("b_dt", 2),
                  ("D", 2), ("b1", 4), ("A_log", 32), ("bg", EXPERTS), ("desc", EXPERTS)):
    COLS[_name] = (_at, _n)
    _at += _n
NCOLS = _at


def gnn_mamba_moe(nc, x_rows, x_cols, adj, vecs, consts, sel, gcn_w, w_in, w_xp, w_dt, w_out, W1, Wg, Wd, bd, out):
    J = x_rows.shape[1]
    N = x_cols.shape[1]
    TILES = N // T
    GROUPS = J // GROUP
    BLOCKS = T // P
    assert TILES % 2 == 0 and TILES >= 6 and GROUPS % RING == 0 and GROUP * GROUPS == J

    with ExitStack() as ctx:
        def sb(name, shape, dt=F32):
            return ctx.enter_context(nc.sbuf_tensor(name, shape, dt))

        def bank(name, n=1):
            return ctx.enter_context(nc.psum_tensor(name, [P, n, T], F32))

        vec_sb = sb("vec_sb", [P, NCOLS])
        const_sb = sb("const_sb", [P, 3, P])
        ident, center, mean = const_sb[:, 0, :], const_sb[:, 1, :], const_sb[:, 2, :]
        sel_sb = sb("sel_sb", [96, 32], BF16)
        gcn_sb = sb("gcn_sb", [P, P])
        win_sb = sb("win_sb", [P, 4, P])
        wxp_sb = sb("wxp_sb", [P, 2, 96])
        rows_w = sb("rows_w", [72, 2, P])
        wdt_sb, bd_sb = rows_w[0:8], rows_w[64:72, 0]
        wout_sb = sb("wout_sb", [P, 2, P])
        w1_sb = sb("w1_sb", [P, 4, P])
        wg_sb = sb("wg_sb", [P, 4, EXPERTS])
        wd_sb = sb("wd_sb", [P, 4, EXPERTS, P])
        negA = sb("negA", [P, 2, SLOTS])
        xz_bias = sb("xz_bias", [P, 4])
        eps_col = sb("eps_col", [P, 1])

        nodes = sb("nodes", [P, J, P])
        row_sum = sb("row_sum", [P, J])
        row_rstd = sb("row_rstd", [P, J])
        ring = sb("ring", [P, RING, GROUP, T])

        front_a = sb("front_a", [P, T])
        front_b = sb("front_b", [P, T])
        conv_in = sb("conv_in", [P, 2, TAPS - 1 + T])
        z_sb = sb("z_sb", [P, 2, 2, T])
        u_sb = sb("u_sb", [P, 2, 2, T])
        soft = sb("soft", [P, 2, T])
        dt_sb = sb("dt_sb", [P, 2, 2, T])
        dtu_sb = sb("dtu_sb", [P, 2, 2, T])
        rows_sb = sb("rows_sb", [72, T])
        dt_low, bc_rest, coef_t = rows_sb[0:8, :], rows_sb[32:64, :], rows_sb[64:72, :]
        bc_parts = sb("bc_parts", [96, 2, T], BF16)

        decay = sb("decay", [P, 2, 2, T])
        inject = sb("inject", [P, 3, 2, T])
        hidden = sb("hidden", [P, 2, 2, T])
        c_wide = sb("c_wide", [P, 2, T])
        h_c = sb("h_c", [P, 2, 2, T])
        state = sb("state", [P, 2, SLOTS])
        y_sum = sb("y_sum", [P, 2, T])
        y_gated = sb("y_gated", [P, 2, T])

        x_tile = sb("x_tile", [P, T])
        x1 = sb("x1", [P, T])
        ffn_a = sb("ffn_a", [P, T])
        ffn_b = sb("ffn_b", [P, T])
        H = sb("H", [P, 4, T])
        logit = sb("logit", [P, BLOCKS, EXPERTS])
        pick = sb("pick", [P, BLOCKS, EXPERTS])
        expo = sb("expo", [P, BLOCKS, EXPERTS])
        coef = sb("coef", [P, BLOCKS, EXPERTS])
        top = sb("top", [P, 4, BLOCKS])
        out_sb = sb("out_sb", [P, BLOCKS, P])
        odd_acc = sb("odd_acc", [P, P])

        ps_adj = bank("ps_adj")
        ps_b = bank("ps_b", 2)
        ps_c = bank("ps_c")
        ps_f = bank("ps_f", 2)
        ps_y = bank("ps_y", 2)

        def vec(name, j=0, n=1):
            first = COLS[name][0] + j
            return vec_sb[:, first:first + n]

        def scratch(e, n):
            return (hidden, h_c)[e].rearrange("p a b n -> p (a b n)")[:, 0:n * P].rearrange("p (j d) -> p j d", d=P)

        def picks(row):
            return sel_sb[:, row:row + 1].broadcast_to([96, P])

        def over_halves(ap):
            return ap.unsqueeze(1).broadcast_to([P, 2, T])

        def over_experts(ap):
            return ap.unsqueeze(2).broadcast_to([P, BLOCKS, EXPERTS])

        def over_blocks(ap):
            return ap.unsqueeze(1).broadcast_to([P, BLOCKS, EXPERTS])

        PER = {}

        def sem(name, per=1):
            s = ctx.enter_context(nc.semaphore(name))
            PER[name] = per
            return s

        weights_in = sem("weights_in")
        node_in = [sem(f"node_in{n}") for n in range(4)]
        ring_in = [sem(f"ring_in{r}") for r in range(RING)]
        adj_used = sem("adj_used", GROUPS)
        start_v, start_a, start_p = sem("start_v"), sem("start_a"), sem("start_p")
        node_sum, node_cen, node_sq, node_var, node_ready = (
            sem("node_sum"), sem("node_cen"), sem("node_sq"), sem("node_var"), sem("node_ready"))
        node_ln, node_rstd = sem("node_ln"), sem("node_rstd")

        agg_ready, gcn_done, gcn_ready = sem("agg_ready"), sem("gcn_done"), sem("gcn_ready")
        cen_done, sq_ready, var_done = sem("cen_done"), sem("sq_ready"), sem("var_done")
        ln_ready, rstd_ready, hn_ready = sem("ln_ready"), sem("rstd_ready"), sem("hn_ready")
        xz_done, xz_ready, tail_ready = sem("xz_done", 4), sem("xz_ready", 4), sem("tail_ready")
        conv_step = sem("conv_step", 2 * TAPS)
        u_ready, dbc_done = sem("u_ready"), sem("dbc_done")
        hi_ready, low_ready, rest_ready, mid_ready, lo_ready = (
            sem("hi_ready"), sem("low_ready"), sem("rest_ready"), sem("mid_ready"), sem("lo_ready"))
        dt_done, clamp_ready, exp_ready, soft_ready, dt_ready, dtu_ready = (
            sem("dt_done", 2), sem("clamp_ready", 2), sem("exp_ready", 2), sem("soft_ready", 2),
            sem("dt_ready", 2), sem("dtu_ready"))

        b_done, c_done, c_ready = sem("b_done", SLOTS), sem("c_done", SLOTS), sem("c_ready", SLOTS)
        decay_ready, inject_ready, scan_ready = (
            sem("decay_ready", SLOTS), sem("inject_ready", SLOTS), sem("scan_ready", SLOTS))
        hc_ready, state_ready, y_step = sem("hc_ready", SLOTS), sem("state_ready", SLOTS), sem("y_step", SLOTS)

        y_ready, wout_done, x_in, x1_ready = sem("y_ready"), sem("wout_done"), sem("x_in", 16), sem("x1_ready")
        cen2_done, sq2_ready, var2_done = sem("cen2_done"), sem("sq2_ready"), sem("var2_done")
        ln2_ready, rstd2_ready, xn_ready = sem("ln2_ready"), sem("rstd2_ready"), sem("xn_ready")
        h_done, h_ready, logit_done = sem("h_done", 4), sem("h_ready", 4), sem("logit_done")
        gate_step = sem("gate_step", 9)
        expo_ready, coef_t_done, coef_t_ready = sem("expo_ready"), sem("coef_t_done"), sem("coef_t_ready")
        base_done, base_ready = sem("base_done"), sem("base_ready")
        yexp_done, acc_step, out_done = sem("yexp_done", 8), sem("acc_step", 9 * BLOCKS), sem("out_done", 16)

        class Count:

            def __init__(self, eng, i):
                self.eng, self.i, self.times = eng, i, {}

            def times_of(self, per):
                if isinstance(self.i, int) or per == 1:
                    return self.i * per
                if per not in self.times:
                    self.times[per] = self.eng.snap(self.i * per)
                return self.times[per]

            def wait(self, s, d, n):
                per = PER[s.name]
                v = self.times_of(per) + (d * per + n)
                if not isinstance(v, int) or v > 0:
                    self.eng.wait_ge(s, v)

        def stages(i):
            live = lambda k: 0 <= k < TILES
            return dict(adjacency=live(i + 2), front=live(i + 1), mamba=live(i), ffn=live(i - 1), experts=live(i - 2))

        ALL = dict(adjacency=True, front=True, mamba=True, ffn=True, experts=True)

        def bodies(eng, body):
            for i in range(-2, 2):
                body(i, i % 2, **stages(i))
            with eng.Fori(2, TILES - 2, 2) as i:
                body(i, 0, **ALL)
                body(i + 1, 1, **ALL)
            for i in range(TILES - 2, TILES + 2):
                body(i, i % 2, **stages(i))

        FIRST_ADJ = 4

        def adj_blocks(s):
            if s < FIRST_ADJ:
                return range(0)
            n = SLOTS - FIRST_ADJ
            return range(J * (s - FIRST_ADJ) // n, J * (s + 1 - FIRST_ADJ) // n)

        def new_states(s):
            return (0, 1) if s == 0 else (s + 1,) if s + 1 < SLOTS else ()

        block = ctx.enter_context(nc.Block())

        @block.sync
        def _(sp):
            def load(k, src, g, used):
                dma = sp.dma_start(ring[:, g % RING], src)
                if used is not None:
                    dma.wait_op(adj_used, used, "sem-ge")
                dma.then_inc(ring_in[g % RING], 16)

            for g in range(GROUPS):
                load(0, adj[0, g], g, g - RING + 1 if g >= RING else None)
            with sp.Fori(1, TILES) as k:
                for g in range(GROUPS):
                    used = sp.lower_val(k * GROUPS + (g - RING + 1))
                    load(k, adj[bass.ds(k, 1), g].rearrange("a p c n -> p (a c) n"), g, used)

        @block.gpsimd
        def _(pool):
            def body(i, p, adjacency, front, mamba, ffn, experts):
                c = Count(pool, i)
                if not mamba:
                    return
                for s in range(SLOTS):
                    c.wait(scan_ready, 0, s + 1)
                    c.wait(c_ready, 0, s + 1)
                    c.wait(y_step, 0, s - 1)
                    nc.gpsimd.tensor_tensor(h_c[:, s % 2], hidden[:, s % 2], over_halves(c_wide[:, s % 2]),
                                            ALU.mult).then_inc(hc_ready, 1)
                    nc.gpsimd.tensor_copy(state[:, :, s:s + 1],
                                          hidden[:, s % 2, :, T - 1:T]).then_inc(state_ready, 1)

            bodies(pool, body)

        @block.scalar
        def _(act):
            def weight(dst, src):
                act.dma_start(dst, src).then_inc(weights_in, 16)

            quarter = J // 4
            for q in range(4):
                act.dma_start(nodes[:, q * quarter:(q + 1) * quarter], x_rows[:, q * quarter:(q + 1) * quarter]
                              ).then_inc(node_in[q], 16)
            for dst, src in ((vec_sb, vecs), (const_sb, consts), (sel_sb, sel), (gcn_sb, gcn_w), (win_sb, w_in),
                             (wxp_sb, w_xp), (wdt_sb, w_dt), (wout_sb, w_out), (w1_sb, W1), (wg_sb, Wg),
                             (wd_sb, Wd), (bd_sb, bd)):
                weight(dst if isinstance(dst, bass.AP) else dst[:], src)
            act.preload_act_table_set(EXP_LN_SET)
            for q in range(4):
                for e in range(2):
                    act.wait_ge(node_cen, 2 * q + e + 1)
                    if 2 * q + e >= 2:
                        act.wait_ge(node_var, 2 * q + e - 1)
                    first = q * quarter + e * (quarter // 2)
                    nc.scalar.activation(scratch(e, quarter // 2), nodes[:, first:first + quarter // 2],
                                         ACT.Square).then_inc(node_sq, 1)
                act.wait_ge(node_var, 2 * q + 2)
                part = row_rstd[:, q * quarter:(q + 1) * quarter]
                nc.scalar.activation(part, part, ACT.Ln, bias=eps_col[:, 0:1], scale=1.0 / P).then_inc(node_ln, 1)
                act.wait_ge(node_ln, q + 1)
                nc.scalar.activation(part, part, ACT.Exp, scale=-0.5).then_inc(node_rstd, 1)
            act.wait_ge(weights_in, 16 * 12)
            nc.scalar.activation(negA[:].rearrange("p a b -> p (a b)"), vec("A_log", 0, 32), ACT.Exp
                                 ).then_inc(start_a, 1)
            act.wait_ge(start_p, 1)
            nc.scalar.copy(xz_bias[:], ps_y[:, 0, 0:4]).then_inc(start_a, 1)
            act.wait_ge(start_a, 2)
            act.wait_ge(start_v, 2)

            def body(i, p, adjacency, front, mamba, ffn, experts):
                c = Count(act, i)
                q = 1 - p
                for s in range(SLOTS):
                    if mamba:
                        for t in new_states(s):
                            c.wait(c_done, 0, t + 1)
                            c.wait(hc_ready, 0, t - 1)
                            nc.scalar.copy(c_wide[:, t % 2], ps_c[:, 0]).then_inc(c_ready, 1)
                            if t == 0:
                                c.wait(dt_ready, 0, 2)
                            c.wait(scan_ready, 0, t - 1)
                            nc.scalar.activation(decay[:, t % 2, 0], dt_sb[:, p, 0], ACT.Exp, scale=negA[:, 0, t:t + 1])
                            nc.scalar.activation(decay[:, t % 2, 1], dt_sb[:, p, 1], ACT.Exp,
                                                 scale=negA[:, 1, t:t + 1]).then_inc(decay_ready, 1)
                    if front and s == 0:
                        c.wait(adj_used, 1, GROUPS)
                        c.wait(xz_done, 1, 0)
                        nc.scalar.copy(front_a[:], ps_adj[:, 0]).then_inc(agg_ready, 1)
                    if ffn and s == 0:
                        c.wait(x1_ready, -1, 0)
                        act.dma_start(x_tile[:], x_cols[:, bass.ds((i - 1) * T, T)]).then_inc(x_in, 16)
                    if front and s == 1:
                        c.wait(gcn_done, 1, 1)
                        nc.scalar.activation(front_b[:], ps_f[:, 0], ACT.Relu, bias=vec("gcn_b")
                                             ).then_inc(gcn_ready, 1)
                    if front and s == 2:
                        c.wait(cen_done, 1, 1)
                        nc.scalar.activation(front_a[:], ps_f[:, 0], ACT.Square).then_inc(sq_ready, 1)
                    if front and s == 3:
                        c.wait(var_done, 1, 1)
                        nc.scalar.activation(front_b[:], ps_f[:, 1], ACT.Ln, bias=eps_col[:, 0:1]).then_inc(ln_ready, 1)
                        c.wait(ln_ready, 1, 1)
                        nc.scalar.activation(front_b[:], front_b[:], ACT.Exp, scale=-0.5).then_inc(rstd_ready, 1)
                    if front and s == 5:
                        c.wait(conv_step, 1, 0)
                        nc.scalar.copy(conv_in[:, :, 0:TAPS - 1], conv_in[:, :, T:T + TAPS - 1]
                                       ).then_inc(tail_ready, 1)
                        c.wait(tail_ready, 1, 1)
                        for h in range(2):
                            c.wait(xz_done, 1, h + 1)
                            nc.scalar.activation(conv_in[:, h, TAPS - 1:], ps_f[:, h], ACT.Identity,
                                                 bias=xz_bias[:, h:h + 1]).then_inc(xz_ready, 1)
                    if front and s == 6:
                        c.wait(y_ready, -1, 1)
                        for h in range(2):
                            c.wait(xz_done, 1, h + 3)
                            nc.scalar.activation(z_sb[:, q, h], ps_f[:, h], ACT.Identity,
                                                 bias=xz_bias[:, h + 2:h + 3]).then_inc(xz_ready, 1)
                    if ffn and s == 6:
                        c.wait(cen2_done, -1, 1)
                        nc.scalar.activation(ffn_a[:], ps_y[:, 1], ACT.Square).then_inc(sq2_ready, 1)
                    if ffn and s == 7:
                        c.wait(var2_done, -1, 1)
                        nc.scalar.activation(ffn_b[:], ps_y[:, 0], ACT.Ln, bias=eps_col[:, 0:1]).then_inc(ln2_ready, 1)
                        c.wait(ln2_ready, -1, 1)
                        nc.scalar.activation(ffn_b[:], ffn_b[:], ACT.Exp, scale=-0.5).then_inc(rstd2_ready, 1)
                    if experts and s == 6:
                        c.wait(acc_step, -2, 9 * BLOCKS)
                        act.dma_start(out[bass.ds((i - 2) * T, T), :].rearrange("(b p) c -> p b c", p=P),
                                      out_sb[:]).then_inc(out_done, 16)
                    if front and s == 9:
                        c.wait(conv_step, 1, 2 * TAPS)
                        nc.scalar.activation(u_sb[:, q], u_sb[:, q], ACT.Silu)
                        c.wait(xz_ready, 1, 4)
                        nc.scalar.activation(z_sb[:, q], z_sb[:, q], ACT.Silu).then_inc(u_ready, 1)
                    if ffn and s == 10:
                        c.wait(yexp_done, -1, 0)
                        for k in range(4):
                            c.wait(h_done, -1, k + 1)
                            nc.scalar.activation(H[:, k], ps_y[:, k % 2], ACT.Gelu, bias=vec("b1", k)
                                                 ).then_inc(h_ready, 1)
                    if (front and s == 9 and not ffn) or (ffn and s == 10):
                        act.preload_act_table_set(EXP_LN_SET)
                    if front and s == 10:
                        c.wait(dbc_done, 1, 1)
                        nc.scalar.copy(bc_parts[0:32, q], ps_f[0:32, 0]).then_inc(hi_ready, 1)
                        nc.scalar.copy(dt_low, ps_f[64:72, 0]).then_inc(low_ready, 1)
                    if front and s == 11:
                        c.wait(rest_ready, 1, 1)
                        nc.scalar.copy(bc_parts[32:64, q], bc_rest).then_inc(mid_ready, 1)
                    if front and s == 12:
                        for h in range(2):
                            c.wait(clamp_ready, 1, h + 1)
                            nc.scalar.activation(soft[:, h], soft[:, h], ACT.Exp).then_inc(exp_ready, 1)
                        for h in range(2):
                            c.wait(exp_ready, 1, h + 1)
                            nc.scalar.activation(soft[:, h], soft[:, h], ACT.Ln, bias=1.0).then_inc(soft_ready, 1)
                    if ffn and s == 13:
                        c.wait(gate_step, -1, 3)
                        nc.scalar.activation(expo[:], logit[:], ACT.Exp).then_inc(expo_ready, 1)
                    if ffn and s == 14:
                        c.wait(coef_t_done, -1, 1)
                        nc.scalar.copy(coef_t, ps_y[0:EXPERTS, 0]
                                       ).then_inc(coef_t_ready, 1)
                    if ffn and s == 15:
                        c.wait(base_done, -1, 1)
                        c.wait(out_done, -1, 0)
                        nc.scalar.copy(out_sb[:].rearrange("p b c -> p (b c)"), ps_y[:, 1]).then_inc(base_ready, 1)

            bodies(act, body)
            act.wait_ge(out_done, 16 * TILES)

        @block.vector
        def _(dve):
            nc.vector.memset(state[:], 0.0).then_inc(start_v, 1)
            nc.vector.memset(conv_in[:], 0.0).then_inc(start_v, 1)
            nc.vector.memset(eps_col[:], EPS).then_inc(start_v, 1)
            quarter = J // 4
            half = quarter // 2

            def rows(ap, first):
                return ap[:, first:first + half].unsqueeze(2).broadcast_to([P, half, P])

            for e in range(8):
                first = e * half
                block_ = nodes[:, first:first + half]
                if e % 2 == 0:
                    dve.wait_ge(node_in[e // 2], 16)
                nc.vector.reduce_sum(row_sum[:, first:first + half], block_, AX).then_inc(node_sum, 1)
                dve.wait_ge(node_sum, e + 1)
                nc.vector.scalar_tensor_tensor(out=block_, in0=rows(row_sum, first), scalar=-1.0 / P, in1=block_,
                                               op0=ALU.mult, op1=ALU.add).then_inc(node_cen, 1)
                dve.wait_ge(node_sq, e + 1)
                nc.vector.reduce_sum(row_rstd[:, first:first + half], scratch(e % 2, half), AX).then_inc(node_var, 1)
                if e % 2:
                    for f in (first - half, first):
                        if f == first - half:
                            dve.wait_ge(node_rstd, e // 2 + 1)
                        nc.vector.tensor_tensor(nodes[:, f:f + half], nodes[:, f:f + half], rows(row_rstd, f),
                                                ALU.mult).then_inc(node_ready, 1)
            dve.wait_ge(weights_in, 16 * 12)
            dve.wait_ge(start_a, 1)
            nc.vector.tensor_scalar_mul(negA[:], negA[:], -1.0).then_inc(start_v, 1)
            dve.wait_ge(start_p, 1)
            nc.vector.tensor_scalar_mul(win_sb[:], win_sb[:], vec("ln_g")).then_inc(start_v, 1)
            dve.wait_ge(start_v, 5)

            def body(i, p, adjacency, front, mamba, ffn, experts):
                c = Count(dve, i)
                q = 1 - p
                for s in range(SLOTS):
                    if mamba:
                        for t in new_states(s):
                            if t == 0:
                                c.wait(dtu_ready, 0, 1)
                            c.wait(b_done, 0, t + 1)
                            c.wait(scan_ready, 0, t - 2 if t else 0)
                            nc.vector.tensor_tensor(inject[:, t % 3], dtu_sb[:, p], over_halves(ps_b[:, t % 2]),
                                                    ALU.mult).then_inc(inject_ready, 1)
                    if ffn and s < 2:
                        t = SLOTS - 2 + s
                        c.wait(hc_ready, -1, t + 1)
                        c.wait(y_step, -1, t)
                        nc.vector.tensor_tensor(y_sum[:], y_sum[:], h_c[:, t % 2], ALU.add).then_inc(y_step, 1)
                    if ffn and s == 1:
                        c.wait(y_step, -1, SLOTS)
                        c.wait(wout_done, -1, 0)
                        nc.vector.tensor_tensor(y_gated[:], y_sum[:], z_sb[:, q], ALU.mult).then_inc(y_ready, 1)
                    if mamba:
                        c.wait(decay_ready, 0, s + 1)
                        c.wait(inject_ready, 0, s + 1)
                        c.wait(state_ready, 0, s - 1)
                        for h in range(2):
                            scan = nc.vector.tensor_tensor_scan(hidden[:, s % 2, h], decay[:, s % 2, h],
                                                                inject[:, s % 3, h], state[:, h, s:s + 1],
                                                                ALU.mult, ALU.add)
                        scan.then_inc(scan_ready, 1)
                        if s == 2:
                            c.wait(hc_ready, 0, 1)
                            c.wait(u_ready, 0, 1)
                            c.wait(y_ready, 0, 0)
                            for h in range(2):
                                step = nc.vector.scalar_tensor_tensor(
                                    out=y_sum[:, h], in0=u_sb[:, p, h], scalar=vec("D", h), in1=h_c[:, 0, h],
                                    op0=ALU.mult, op1=ALU.add)
                            step.then_inc(y_step, 1)
                        elif s > 2:
                            c.wait(hc_ready, 0, s - 1)
                            c.wait(y_step, 0, s - 2)
                            nc.vector.tensor_tensor(y_sum[:], y_sum[:], h_c[:, s % 2], ALU.add).then_inc(y_step, 1)
                    if experts and 1 <= s <= BLOCKS:
                        b = s - 1
                        if b == 0:
                            c.wait(base_ready, -2, 1)
                        for e in range(EXPERTS):
                            if e % 4 == 0:
                                c.wait(yexp_done, -2, 2 * b + e // 4 + 1)
                            c.wait(acc_step, -2, 9 * b + e - 1 if e > 1 else 9 * b)
                            src = ps_y[:, e // 4, (e % 4) * P:(e % 4 + 1) * P]
                            w = coef[:, b, e:e + 1]
                            if e == 1:
                                step = nc.vector.tensor_scalar_mul(odd_acc[:], src, w)
                            else:
                                acc = odd_acc[:] if e % 2 else out_sb[:, b]
                                step = nc.vector.scalar_tensor_tensor(out=acc, in0=src, scalar=w, in1=acc,
                                                                      op0=ALU.mult, op1=ALU.add)
                            step.then_inc(acc_step, 1)
                        c.wait(acc_step, -2, 9 * b + 8)
                        nc.vector.tensor_tensor(out_sb[:, b], out_sb[:, b], odd_acc[:], ALU.add
                                                ).then_inc(acc_step, 1)
                    if front and s == 4:
                        c.wait(rstd_ready, 1, 1)
                        nc.vector.tensor_tensor(front_a[:], ps_f[:, 0], front_b[:], ALU.mult).then_inc(hn_ready, 1)
                    if ffn and s == 5:
                        c.wait(wout_done, -1, 1)
                        c.wait(x_in, -1, 16)
                        c.wait(base_done, -1, 0)
                        nc.vector.tensor_tensor(x1[:], ps_y[:, 0], x_tile[:], ALU.add).then_inc(x1_ready, 1)
                    if front and s == 7:
                        c.wait(xz_ready, 1, 2)
                        for k in range(TAPS):
                            for h in range(2):
                                src = conv_in[:, h, k:k + T]
                                w = vec("conv_w", TAPS * h + k)
                                if k == 0:
                                    step = nc.vector.tensor_scalar(u_sb[:, q, h], src, w, vec("conv_b", h),
                                                                   ALU.mult, ALU.add)
                                else:
                                    c.wait(conv_step, 1, 2 * k + h - 1)
                                    step = nc.vector.scalar_tensor_tensor(
                                        out=u_sb[:, q, h], in0=src, scalar=w, in1=u_sb[:, q, h],
                                        op0=ALU.mult, op1=ALU.add)
                                step.then_inc(conv_step, 1)
                    if ffn and s == 8:
                        c.wait(rstd2_ready, -1, 1)
                        nc.vector.tensor_tensor(ffn_a[:], ps_y[:, 1], ffn_b[:], ALU.mult).then_inc(xn_ready, 1)
                    if front and s == 11:
                        c.wait(hi_ready, 1, 1)
                        c.wait(lo_ready, 1, 0)
                        nc.vector.tensor_tensor(bc_rest, ps_f[0:32, 0], bc_parts[0:32, q], ALU.subtract
                                                ).then_inc(rest_ready, 1)
                    if front and s == 12:
                        for h in range(2):
                            c.wait(dt_done, 1, h + 1)
                            c.wait(dt_ready, 1, 0)
                            nc.vector.tensor_scalar(soft[:, h], ps_f[:, 1 - h], vec("b_dt", h), CLAMP,
                                                    ALU.add, ALU.min).then_inc(clamp_ready, 1)
                        c.wait(mid_ready, 1, 1)
                        nc.vector.tensor_tensor(bc_parts[64:96, q], bc_rest, bc_parts[32:64, q],
                                                ALU.subtract).then_inc(lo_ready, 1)
                    if ffn and s == 12:
                        c.wait(logit_done, -1, 1)
                        c.wait(gate_step, -1, 0)
                        nc.vector.tensor_tensor(logit[:], ps_y[:, 0, 0:BLOCKS * EXPERTS].rearrange(
                            "p (b e) -> p b e", b=BLOCKS), over_blocks(vec("bg", 0, EXPERTS)), ALU.add
                            ).then_inc(gate_step, 1)
                        c.wait(gate_step, -1, 1)
                        nc.vector.reduce_max(top[:, 0], logit[:], AX).then_inc(gate_step, 1)
                        c.wait(gate_step, -1, 2)
                        nc.vector.tensor_tensor(logit[:], logit[:], over_experts(top[:, 0]), ALU.subtract
                                                ).then_inc(gate_step, 1)
                    if ffn and s == 13:
                        c.wait(gate_step, -1, 3)
                        nc.vector.scalar_tensor_tensor(out=pick[:], in0=logit[:], scalar=0.0,
                                                       in1=over_blocks(vec("desc", 0, EXPERTS)), op0=ALU.is_ge,
                                                       op1=ALU.mult).then_inc(gate_step, 1)
                        c.wait(gate_step, -1, 4)
                        nc.vector.reduce_max(top[:, 1], pick[:], AX).then_inc(gate_step, 1)
                        c.wait(gate_step, -1, 5)
                        nc.vector.tensor_tensor(pick[:], over_blocks(vec("desc", 0, EXPERTS)), over_experts(top[:, 1]),
                                                ALU.is_equal).then_inc(gate_step, 1)
                        c.wait(expo_ready, -1, 1)
                        nc.vector.reduce_sum(top[:, 2], expo[:], AX).then_inc(gate_step, 1)
                        c.wait(gate_step, -1, 7)
                        nc.vector.reciprocal(top[:, 3], top[:, 2]).then_inc(gate_step, 1)
                        c.wait(gate_step, -1, 8)
                        nc.vector.tensor_tensor(coef[:], pick[:], over_experts(top[:, 3]), ALU.mult
                                                ).then_inc(gate_step, 1)
                    if front and s == 14:
                        for h in range(2):
                            c.wait(soft_ready, 1, h + 1)
                            nc.vector.scalar_tensor_tensor(out=dt_sb[:, q, h], in0=ps_f[:, 1 - h],
                                                           scalar=vec("b_dt", h), in1=soft[:, h], op0=ALU.add,
                                                           op1=ALU.max).then_inc(dt_ready, 1)
                        c.wait(dt_ready, 1, 2)
                        c.wait(u_ready, 1, 1)
                        nc.vector.tensor_tensor(dtu_sb[:, q], dt_sb[:, q], u_sb[:, q], ALU.mult
                                                ).then_inc(dtu_ready, 1)

            bodies(dve, body)

        @block.tensor
        def _(pe):
            def product(dst, pairs):
                for n, (stationary, moving) in enumerate(pairs):
                    last = nc.tensor.matmul(dst, stationary, moving, start=(n == 0), stop=(n == len(pairs) - 1))
                return last

            pe.wait_ge(weights_in, 16 * 12)
            for k in range(4):
                last = nc.tensor.matmul(ps_y[:, 0, k:k + 1], win_sb[:, k], vec("ln_b"), start=True, stop=True)
            last.then_inc(start_p, 1)
            pe.wait_ge(start_a, 2)
            pe.wait_ge(start_v, 5)

            def body(i, p, adjacency, front, mamba, ffn, experts):
                c = Count(pe, i)
                q = 1 - p
                for s in range(SLOTS):
                    if mamba:
                        for t in new_states(s):
                            if t == 0:
                                c.wait(lo_ready, 0, 1)
                            c.wait(inject_ready, 0, t - 1)
                            nc.tensor.matmul(ps_b[:, t % 2], picks(t), bc_parts[:, p], start=True,
                                             stop=True).then_inc(b_done, 1)
                            c.wait(c_ready, 0, t)
                            nc.tensor.matmul(ps_c[:, 0], picks(SLOTS + t), bc_parts[:, p], start=True,
                                             stop=True).then_inc(c_done, 1)
                    if experts and s < BLOCKS:
                        if s == 0:
                            c.wait(base_ready, -2, 1)
                        for g in range(2):
                            if s:
                                c.wait(acc_step, -2, 9 * (s - 1) + (4 if g == 0 else 8))
                            product(ps_y[:, g], [(H[:, k, s * P:(s + 1) * P],
                                                  wd_sb[:, k, 4 * g:4 * g + 4].rearrange("p e c -> p (e c)"))
                                                 for k in range(4)]).then_inc(yexp_done, 1)
                    if front and s == 1:
                        c.wait(agg_ready, 1, 1)
                        c.wait(dt_ready, 1, 0)
                        product(ps_f[:, 0], [(gcn_sb[:], front_a[:])]).then_inc(gcn_done, 1)
                    if front and s == 2:
                        c.wait(gcn_ready, 1, 1)
                        product(ps_f[:, 0], [(center, front_b[:])]).then_inc(cen_done, 1)
                    if front and s == 3:
                        c.wait(sq_ready, 1, 1)
                        product(ps_f[:, 1], [(mean, front_a[:])]).then_inc(var_done, 1)
                    if ffn and s == 4:
                        c.wait(y_ready, -1, 1)
                        c.wait(acc_step, -1, 0)
                        product(ps_y[:, 0], [(wout_sb[:, h], y_gated[:, h]) for h in range(2)]
                                ).then_inc(wout_done, 1)
                    if front and s == 5:
                        c.wait(hn_ready, 1, 1)
                        for k in range(2):
                            product(ps_f[:, k], [(win_sb[:, k], front_a[:])]).then_inc(xz_done, 1)
                    if front and s == 6:
                        for k in range(2):
                            c.wait(xz_ready, 1, k + 1)
                            product(ps_f[:, k], [(win_sb[:, 2 + k], front_a[:])]).then_inc(xz_done, 1)
                    if ffn and s == 6:
                        c.wait(x1_ready, -1, 1)
                        product(ps_y[:, 1], [(center, x1[:])]).then_inc(cen2_done, 1)
                    if ffn and s == 7:
                        c.wait(sq2_ready, -1, 1)
                        product(ps_y[:, 0], [(mean, ffn_a[:])]).then_inc(var2_done, 1)
                    if ffn and s == 9:
                        c.wait(xn_ready, -1, 1)
                        for k in range(2):
                            product(ps_y[:, k], [(w1_sb[:, k], ffn_a[:])]).then_inc(h_done, 1)
                    if front and s == 10:
                        c.wait(u_ready, 1, 1)
                        product(ps_f[0:96, 0], [(wxp_sb[:, h], u_sb[:, q, h]) for h in range(2)]
                                ).then_inc(dbc_done, 1)
                    if ffn and s == 10:
                        for k in range(2):
                            c.wait(h_ready, -1, k + 1)
                            product(ps_y[:, k], [(w1_sb[:, 2 + k], ffn_a[:])]).then_inc(h_done, 1)
                    if front and s == 11:
                        c.wait(low_ready, 1, 1)
                        product(ps_f[:, 1], [(wdt_sb[:, 0], dt_low)]).then_inc(dt_done, 1)
                        c.wait(rest_ready, 1, 1)
                        product(ps_f[:, 0], [(wdt_sb[:, 1], dt_low)]).then_inc(dt_done, 1)
                    if ffn and s == 11:
                        c.wait(h_ready, -1, 4)
                        for b in range(BLOCKS):
                            last = product(ps_y[:, 0, b * EXPERTS:(b + 1) * EXPERTS],
                                           [(H[:, k, b * P:(b + 1) * P], wg_sb[:, k]) for k in range(4)])
                        last.then_inc(logit_done, 1)
                    if ffn and s == 14:
                        c.wait(gate_step, -1, 9)
                        for b in range(BLOCKS):
                            last = product(ps_y[0:EXPERTS, 0, b * P:(b + 1) * P], [(coef[:, b], ident)])
                        last.then_inc(coef_t_done, 1)
                    if ffn and s == 15:
                        c.wait(coef_t_ready, -1, 1)
                        for b in range(BLOCKS):
                            last = product(ps_y[:, 1, b * P:(b + 1) * P],
                                           [(x1[:, b * P:(b + 1) * P], ident), (coef_t[:, b * P:(b + 1) * P], bd_sb)])
                        last.then_inc(base_done, 1)
                    if adjacency:
                        for m in adj_blocks(s):
                            g = m // GROUP
                            if m == 0:
                                c.wait(agg_ready, 2, 0)
                            if m % GROUP == 0:
                                fills = GROUPS // RING
                                pe.wait_ge(ring_in[g % RING], c.times_of(16 * fills) + (2 * fills + g // RING + 1) * 16)
                                if isinstance(i, int) and i == -2 and m % (J // 8) == 0:
                                    pe.wait_ge(node_ready, m // (J // 8) + 1)
                            last = nc.tensor.matmul(ps_adj[:, 0], nodes[:, m], ring[:, g % RING, m % GROUP],
                                                    start=(m == 0), stop=(m == J - 1))
                            if m % GROUP == GROUP - 1:
                                last.then_inc(adj_used, 1)

            bodies(pe, body)


def kernel(**inputs):
    import ml_dtypes
    import numpy as np
    import concourse.bacc as bacc
    from concourse.bass_utils import run_bass_kernel_spmd

    a = {k.replace("L0_", ""): np.asarray(v) for k, v in inputs.items()}
    x, adj = a["x"], a["adj"]
    N, D = x.shape
    J = N // P

    def halves(v):
        return v.reshape(2, P, -1).transpose(1, 0, 2)

    vecs = np.zeros((P, NCOLS), np.float32)
    for name, v in (("gcn_b", a["gnn_gcn_b"][:, None]), ("ln_g", a["gnn_ln_g"][:, None]),
                    ("ln_b", a["gnn_ln_b"][:, None]), ("conv_w", halves(a["gnn_conv_w"]).reshape(P, -1)),
                    ("conv_b", a["gnn_conv_b"].reshape(2, P).T), ("b_dt", a["gnn_b_dt"].reshape(2, P).T),
                    ("D", a["gnn_D_skip"].reshape(2, P).T), ("b1", a["ffn_b1"].reshape(4, P).T),
                    ("A_log", halves(a["gnn_A_log"]).reshape(P, -1)),
                    ("bg", np.broadcast_to(a["ffn_bg"], (P, EXPERTS))),
                    ("desc", np.broadcast_to(np.arange(EXPERTS, 0, -1, dtype=np.float32), (P, EXPERTS)))):
        first, n = COLS[name]
        vecs[:, first:first + n] = v
    eye = np.eye(P, dtype=np.float32)
    mean = np.full((P, P), 1.0 / P, np.float32)
    consts = np.stack([eye, eye - mean, mean], axis=1)
    sel = np.tile(np.eye(32), (3, 1)).astype(ml_dtypes.bfloat16)
    w_xp = np.zeros((P, 2, 96), np.float32)
    xp = halves(a["gnn_w_xp"])
    w_xp[:, :, 0:32] = xp[:, :, 8:40]
    w_xp[:, :, 64:72] = xp[:, :, 0:8]

    arrays = {
        "x_rows": x.reshape(P, J, D), "x_cols": x.T,
        "adj": adj.reshape(N // T, T, P, J // GROUP, GROUP).transpose(0, 3, 2, 4, 1),
        "vecs": vecs, "consts": consts, "sel": sel, "gcn_w": a["gnn_gcn_w"],
        "w_in": a["gnn_w_in"].reshape(P, 4, P), "w_xp": w_xp, "w_dt": a["gnn_w_dt"].reshape(8, 2, P),
        "w_out": halves(a["gnn_w_out"]), "W1": a["ffn_W1"].reshape(P, 4, P),
        "Wg": a["ffn_Wg"].reshape(4, P, EXPERTS).transpose(1, 0, 2),
        "Wd": a["ffn_Wd"].reshape(EXPERTS, 4, P, P).transpose(2, 1, 0, 3), "bd": a["ffn_bd"],
    }
    arrays = {k: np.ascontiguousarray(v) for k, v in arrays.items()}
    nc = bacc.Bacc("TRN2", target_bir_lowering=False, num_devices=1)
    args = [nc.dram_tensor(k, v.shape, mybir.dt.from_np(v.dtype), kind="ExternalInput").ap()
            for k, v in arrays.items()]
    out = nc.dram_tensor("out", (N, D), F32, kind="ExternalOutput").ap()
    gnn_mamba_moe(nc, *args, out)
    r = run_bass_kernel_spmd(nc, [arrays], core_ids=[0])
    return r.results[0]["out"]
```

```python
from contextlib import ExitStack

import concourse.bass as bass
from concourse import mybir

P = 128
T = 512
SLOTS = 16
GROUP = 2
RING = 4
EPS = 1e-5
CLAMP = 40.0
TAPS = 4
EXPERTS = 8

ALU = mybir.AluOpType
ACT = mybir.ActivationFunctionType
F32 = mybir.dt.float32
F32R = mybir.dt.float32r
BF16 = mybir.dt.bfloat16
AX = mybir.AxisListType.X
EXP_LN_SET = "natural_log_exp_and_others"

COLS = {}
_at = 0
for _name, _n in (("gcn_b", 1), ("ln_g", 1), ("ln_b", 1), ("conv_w", 2 * TAPS), ("conv_b", 2), ("b_dt", 2),
                  ("D", 2), ("b1", 4), ("A_log", 32), ("bg", EXPERTS), ("desc", EXPERTS)):
    COLS[_name] = (_at, _n)
    _at += _n
NCOLS = _at


def gnn_mamba_moe(nc, x_rows, x_cols, adj, vecs, consts, sel, gcn_w, w_in, w_xp, w_dt, w_out, W1, Wg, Wd, bd, out):
    J = x_rows.shape[1]
    N = x_cols.shape[1]
    TILES = N // T
    GROUPS = J // GROUP
    BLOCKS = T // P
    UNITS = BLOCKS * EXPERTS // 2
    assert TILES % 2 == 0 and TILES >= 6 and GROUPS % RING == 0 and GROUP * GROUPS == J

    with ExitStack() as ctx:
        def sb(name, shape, dt=F32):
            return ctx.enter_context(nc.sbuf_tensor(name, shape, dt))

        def bank(name, n=1):
            return ctx.enter_context(nc.psum_tensor(name, [P, n, T], F32))

        vec_sb = sb("vec_sb", [P, NCOLS])
        const_sb = sb("const_sb", [P, 3, P])
        ident, center, mean = const_sb[:, 0, :], const_sb[:, 1, :], const_sb[:, 2, :]
        sel_sb = sb("sel_sb", [96, 32], BF16)
        gcn_sb = sb("gcn_sb", [P, P])
        win_sb = sb("win_sb", [P, 4, P])
        wxp_sb = sb("wxp_sb", [P, 2, 96])
        rows_w = sb("rows_w", [72, 2, P])
        wdt_sb, bd_sb = rows_w[0:8], rows_w[64:72, 0]
        wout_sb = sb("wout_sb", [P, 2, P])
        w1_sb = sb("w1_sb", [P, 4, P])
        wg_sb = sb("wg_sb", [P, 4, EXPERTS])
        wd_parts = sb("wd_parts", [P, 2, 4, EXPERTS, P], F32R)
        negA = sb("negA", [P, 2, SLOTS])
        xz_bias = sb("xz_bias", [P, 4])
        eps_col = sb("eps_col", [P, 1])

        nodes = sb("nodes", [P, J, P])
        row_sum = sb("row_sum", [P, J])
        row_rstd = sb("row_rstd", [P, J])
        ring = sb("ring", [P, RING, GROUP, T])

        front_a = sb("front_a", [P, T])
        front_b = sb("front_b", [P, T])
        conv_in = sb("conv_in", [P, 2, TAPS - 1 + T])
        z_sb = sb("z_sb", [P, 2, 2, T])
        u_sb = sb("u_sb", [P, 2, T])
        soft = sb("soft", [P, 2, T])
        dt_sb = sb("dt_sb", [P, 2, 2, T])
        dtu_sb = sb("dtu_sb", [P, 2, T])
        rows_sb = sb("rows_sb", [72, T])
        dt_low, bc_rest, coef_t = rows_sb[0:8, :], rows_sb[32:64, :], rows_sb[64:72, :]
        bc_parts = sb("bc_parts", [96, 2, T], BF16)

        decay = sb("decay", [P, 2, 2, T])
        inject = sb("inject", [P, 2, 2, T])
        hidden = sb("hidden", [P, 2, 2, T])
        c_wide = sb("c_wide", [P, 2, T])
        h_c = sb("h_c", [P, 2, 2, T])
        state = sb("state", [P, 2, SLOTS])
        y_sum = sb("y_sum", [P, 2, T])
        y_gated = soft

        x_tile = sb("x_tile", [P, T])
        x1 = sb("x1", [P, T])
        ffn_a = sb("ffn_a", [P, T])
        ffn_b = front_b
        H = sb("H", [P, 2, 4, T])
        H_parts = sb("H_parts", [P, 2, 2, 4, P], F32R)
        wd_sb = H[:].rearrange("p a k n -> p (a k n)").rearrange("p (k e c) -> p k e c", k=4, e=EXPERTS)
        logit = sb("logit", [P, BLOCKS, EXPERTS])
        pick = sb("pick", [P, BLOCKS, EXPERTS])
        expo = sb("expo", [P, BLOCKS, EXPERTS])
        coef = sb("coef", [P, 2, BLOCKS, EXPERTS])
        top = sb("top", [P, 4, BLOCKS])
        out_sb = sb("out_sb", [P, 2, BLOCKS, P])
        odd_acc = sb("odd_acc", [P, P])

        ps_adj = bank("ps_adj")
        ps_b = bank("ps_b")
        ps_c = bank("ps_c")
        ps_f = bank("ps_f", 2)
        ps_y = bank("ps_y")
        ps_e = bank("ps_e", 2)

        def vec(name, j=0, n=1):
            first = COLS[name][0] + j
            return vec_sb[:, first:first + n]

        def scratch(e, n):
            return (hidden, h_c)[e].rearrange("p a b n -> p (a b n)")[:, 0:n * P].rearrange("p (j d) -> p j d", d=P)

        def h_bank(k):
            return (ps_f[:, 0], ps_f[:, 1], ps_y[:, 0], ps_f[:, 1])[k]

        def picks(row):
            return sel_sb[:, row:row + 1].broadcast_to([96, P])

        def over_halves(ap):
            return ap.unsqueeze(1).broadcast_to([P, 2, T])

        def over_experts(ap):
            return ap.unsqueeze(2).broadcast_to([P, BLOCKS, EXPERTS])

        def over_blocks(ap):
            return ap.unsqueeze(1).broadcast_to([P, BLOCKS, EXPERTS])

        PER = {}

        def sem(name, per=1):
            s = ctx.enter_context(nc.semaphore(name))
            PER[name] = per
            return s

        weights_in = sem("weights_in")
        node_in = [sem(f"node_in{n}") for n in range(4)]
        ring_in = [sem(f"ring_in{r}") for r in range(RING)]
        adj_used = sem("adj_used", GROUPS)
        start_v, start_a, start_p = sem("start_v"), sem("start_a"), sem("start_p")
        node_sum, node_cen, node_sq, node_var, node_ready = (
            sem("node_sum"), sem("node_cen"), sem("node_sq"), sem("node_var"), sem("node_ready"))
        node_ln, node_rstd = sem("node_ln"), sem("node_rstd")

        agg_ready, gcn_done, gcn_ready = sem("agg_ready"), sem("gcn_done"), sem("gcn_ready")
        cen_done, sq_ready, var_done = sem("cen_done"), sem("sq_ready"), sem("var_done")
        ln_ready, rstd_ready, hn_ready = sem("ln_ready"), sem("rstd_ready"), sem("hn_ready")
        xz_done, xz_ready, tail_ready = sem("xz_done", 4), sem("xz_ready", 4), sem("tail_ready")
        conv_step = sem("conv_step", 2 * TAPS)
        u_ready, dbc_done = sem("u_ready"), sem("dbc_done")
        hi_ready, low_ready, rest_ready, mid_ready, lo_ready = (
            sem("hi_ready"), sem("low_ready"), sem("rest_ready"), sem("mid_ready"), sem("lo_ready"))
        dt_done, clamp_ready, exp_ready, soft_ready, dt_ready, dtu_ready = (
            sem("dt_done", 2), sem("clamp_ready", 2), sem("exp_ready", 2), sem("soft_ready", 2),
            sem("dt_ready", 2), sem("dtu_ready"))

        b_done, c_done, c_ready = sem("b_done", SLOTS), sem("c_done", SLOTS), sem("c_ready", SLOTS)
        decay_ready, inject_ready, scan_ready = (
            sem("decay_ready", SLOTS), sem("inject_ready", SLOTS), sem("scan_ready", SLOTS))
        hc_ready, state_ready, y_step = sem("hc_ready", SLOTS), sem("state_ready", SLOTS), sem("y_step", SLOTS)

        y_ready, wout_done, x_in, x1_ready = sem("y_ready"), sem("wout_done"), sem("x_in", 16), sem("x1_ready")
        cen2_done, sq2_ready, var2_done = sem("cen2_done"), sem("sq2_ready"), sem("var2_done")
        ln2_ready, rstd2_ready, xn_ready = sem("ln2_ready"), sem("rstd2_ready"), sem("xn_ready")
        h_done, h_ready, logit_done = sem("h_done", 4), sem("h_ready", 4), sem("logit_done")
        gate_step = sem("gate_step", 9)
        expo_ready, coef_t_done, coef_t_ready = sem("expo_ready"), sem("coef_t_done"), sem("coef_t_ready")
        base_done, base_ready = sem("base_done"), sem("base_ready")
        hi_split, lo_split = sem("hi_split", BLOCKS), sem("lo_split", BLOCKS)
        yexp_done, acc_step, out_done = sem("yexp_done", UNITS), sem("acc_step", 9 * BLOCKS), [sem("out_done0", 8), sem("out_done1", 8)]
        cen2_kept = sem("cen2_kept")

        class Count:

            def __init__(self, eng, i):
                self.eng, self.i, self.times = eng, i, {}

            def times_of(self, per):
                if isinstance(self.i, int) or per == 1:
                    return self.i * per
                if per not in self.times:
                    self.times[per] = self.eng.snap(self.i * per)
                return self.times[per]

            def value(self, s, d, n):
                v = self.times_of(PER[s.name]) + (d * PER[s.name] + n)
                if isinstance(v, int):
                    return v if v > 0 else None
                return self.eng.lower_val(v)

            def wait(self, s, d, n):
                per = PER[s.name]
                v = self.times_of(per) + (d * per + n)
                if not isinstance(v, int) or v > 0:
                    self.eng.wait_ge(s, v)

        def stages(i):
            live = lambda k: 0 <= k < TILES
            return dict(adjacency=live(i + 2), front=live(i + 1), mamba=live(i), ffn=live(i - 1), experts=live(i - 2))

        ALL = dict(adjacency=True, front=True, mamba=True, ffn=True, experts=True)

        def bodies(eng, body):
            for i in range(-2, 4):
                body(i, i % 2, **stages(i))
            with eng.Fori(4, TILES - 3, 2) as i:
                body(i, 0, **ALL)
                body(i + 1, 1, **ALL)
            for i in range(TILES - 2, TILES + 2):
                body(i, i % 2, **stages(i))

        def adj_blocks(s):
            return range(J * s // SLOTS, J * (s + 1) // SLOTS)

        def next_state(s, mamba, front):
            if s + 1 < SLOTS:
                return ((0, s + 1),) if mamba else ()
            return ((1, 0),) if front else ()

        def next_split(s, ffn, experts):
            if s == 14:
                return ((-1, 0),) if ffn else ()
            return ((-2, s // 4 + 1),) if experts and s % 4 == 2 else ()

        def unit_before(d, b):
            return (d, 4 * (b - 1)) if b >= 2 else (d - 1, 4 * (b + 3))

        block = ctx.enter_context(nc.Block())

        @block.sync
        def _(sp):
            def store(c, i, q):
                summed = c.value(acc_step, -3, 9 * BLOCKS)
                sp.dma_start(out[bass.ds((i - 3) * T, T), :].rearrange("(b p) c -> p b c", p=P), out_sb[:, q]
                             ).wait_op(acc_step, summed, "sem-ge").then_inc(out_done[q], 16)

            def body(i, p, adjacency, front, mamba, ffn, experts):
                c = Count(sp, i)
                for g in range(GROUPS):
                    if adjacency:
                        src = adj[bass.ds(i + 2, 1), g].rearrange("a p c n -> p (a c) n")
                        used = c.value(adj_used, 2, g - RING + 1)
                        dma = sp.dma_start(ring[:, g % RING], src)
                        if used is not None:
                            dma.wait_op(adj_used, used, "sem-ge")
                        dma.then_inc(ring_in[g % RING], 16)
                    if g == GROUPS // 2 and (not isinstance(i, int) or 0 <= i - 3 < TILES):
                        store(c, i, 1 - p)
                    if g == GROUPS - 2 and mamba:
                        used = c.value(xn_ready, 0, 0)
                        dma = sp.dma_start(x_tile[:], x_cols[:, bass.ds(i * T, T)])
                        if used is not None:
                            dma.wait_op(xn_ready, used, "sem-ge")
                        dma.then_inc(x_in, 16)

            bodies(sp, body)
            store(Count(sp, TILES + 2), TILES + 2, 1)
            for q in range(2):
                sp.wait_ge(out_done[q], 16 * TILES // 2)

        @block.gpsimd
        def _(pool):
            def body(i, p, adjacency, front, mamba, ffn, experts):
                c = Count(pool, i)
                q = 1 - p
                for s in range(SLOTS):
                    for d, b in next_split(s, ffn, experts):
                        c.wait(hi_split, d, b + 1)
                        half = (q if d == -1 else p)
                        nc.gpsimd.tensor_tensor(H_parts[:, 1, b % 2], H[:, half, :, b * P:(b + 1) * P],
                                                H_parts[:, 0, b % 2].bitcast(F32), ALU.subtract
                                                ).then_inc(lo_split, 1)
                    if not mamba:
                        continue
                    c.wait(scan_ready, 0, s + 1)
                    c.wait(c_ready, 0, s + 1)
                    c.wait(y_step, 0, s - 1)
                    nc.gpsimd.tensor_tensor(h_c[:, s % 2], hidden[:, s % 2], over_halves(c_wide[:, s % 2]),
                                            ALU.mult).then_inc(hc_ready, 1)
                    nc.gpsimd.tensor_copy(state[:, :, s:s + 1],
                                          hidden[:, s % 2, :, T - 1:T]).then_inc(state_ready, 1)

            bodies(pool, body)

        @block.scalar
        def _(act):
            def weight(dst, src):
                act.dma_start(dst, src).then_inc(weights_in, 16)

            quarter = J // 4
            for q in range(4):
                act.dma_start(nodes[:, q * quarter:(q + 1) * quarter], x_rows[:, q * quarter:(q + 1) * quarter]
                              ).then_inc(node_in[q], 16)
            for dst, src in ((vec_sb, vecs), (const_sb, consts), (sel_sb, sel), (gcn_sb, gcn_w), (win_sb, w_in),
                             (wxp_sb, w_xp), (wdt_sb, w_dt), (wout_sb, w_out), (w1_sb, W1), (wg_sb, Wg),
                             (wd_sb, Wd), (bd_sb, bd)):
                weight(dst if isinstance(dst, bass.AP) else dst[:], src)
            act.preload_act_table_set(EXP_LN_SET)
            for q in range(4):
                for e in range(2):
                    act.wait_ge(node_cen, 2 * q + e + 1)
                    if 2 * q + e >= 2:
                        act.wait_ge(node_var, 2 * q + e - 1)
                    first = q * quarter + e * (quarter // 2)
                    nc.scalar.activation(scratch(e, quarter // 2), nodes[:, first:first + quarter // 2],
                                         ACT.Square).then_inc(node_sq, 1)
                act.wait_ge(node_var, 2 * q + 2)
                part = row_rstd[:, q * quarter:(q + 1) * quarter]
                nc.scalar.activation(part, part, ACT.Ln, bias=eps_col[:, 0:1], scale=1.0 / P).then_inc(node_ln, 1)
                act.wait_ge(node_ln, q + 1)
                nc.scalar.activation(part, part, ACT.Exp, scale=-0.5).then_inc(node_rstd, 1)
            act.wait_ge(weights_in, 16 * 12)
            nc.scalar.activation(negA[:].rearrange("p a b -> p (a b)"), vec("A_log", 0, 32), ACT.Exp
                                 ).then_inc(start_a, 1)
            act.wait_ge(start_p, 1)
            nc.scalar.copy(xz_bias[:], ps_y[:, 0, 0:4]).then_inc(start_a, 1)
            nc.scalar.copy(wd_parts[:, 0], wd_sb).then_inc(start_a, 1)
            act.wait_ge(start_a, 3)
            act.wait_ge(start_v, 2)

            def body(i, p, adjacency, front, mamba, ffn, experts):
                c = Count(act, i)
                q = 1 - p
                for s in range(SLOTS):
                    if front and s == 0:
                        c.wait(adj_used, 1, GROUPS)
                        c.wait(xz_done, 1, 0)
                        nc.scalar.copy(front_a[:], ps_adj[:, 0]).then_inc(agg_ready, 1)
                    if experts and s == 0:
                        c.wait(base_done, -2, 1)
                        c.wait(out_done[p], 0, -16 - 8 * p)
                        nc.scalar.copy(out_sb[:, p].rearrange("p b c -> p (b c)"), ps_y[:, 0]).then_inc(base_ready, 1)
                    if front and s == 1:
                        c.wait(gcn_done, 1, 1)
                        nc.scalar.activation(front_b[:], ps_f[:, 0], ACT.Relu, bias=vec("gcn_b")
                                             ).then_inc(gcn_ready, 1)
                    if front and s == 2:
                        c.wait(cen_done, 1, 1)
                        nc.scalar.activation(front_a[:], ps_f[:, 0], ACT.Square).then_inc(sq_ready, 1)
                    if front and s == 3:
                        c.wait(var_done, 1, 1)
                        nc.scalar.activation(front_b[:], ps_f[:, 1], ACT.Ln, bias=eps_col[:, 0:1]).then_inc(ln_ready, 1)
                        c.wait(ln_ready, 1, 1)
                        nc.scalar.activation(front_b[:], front_b[:], ACT.Exp, scale=-0.5).then_inc(rstd_ready, 1)
                    if ffn and s == 4:
                        c.wait(cen2_done, -1, 1)
                        nc.scalar.activation(ffn_a[:], ps_y[:, 0], ACT.Square).then_inc(sq2_ready, 1)
                        nc.scalar.copy(x_tile[:], ps_y[:, 0]).then_inc(cen2_kept, 1)
                    if ffn and s == 5:
                        c.wait(var2_done, -1, 1)
                        if front:
                            c.wait(hn_ready, 1, 1)
                        nc.scalar.activation(ffn_b[:], ps_y[:, 0], ACT.Ln, bias=eps_col[:, 0:1]).then_inc(ln2_ready, 1)
                        c.wait(ln2_ready, -1, 1)
                        nc.scalar.activation(ffn_b[:], ffn_b[:], ACT.Exp, scale=-0.5).then_inc(rstd2_ready, 1)
                    if front and s == 5:
                        c.wait(conv_step, 1, 0)
                        nc.scalar.copy(conv_in[:, :, 0:TAPS - 1], conv_in[:, :, T:T + TAPS - 1]
                                       ).then_inc(tail_ready, 1)
                        c.wait(tail_ready, 1, 1)
                        for h in range(2):
                            c.wait(xz_done, 1, h + 1)
                            nc.scalar.activation(conv_in[:, h, TAPS - 1:], ps_f[:, h], ACT.Identity,
                                                 bias=xz_bias[:, h:h + 1]).then_inc(xz_ready, 1)
                    if front and s == 6:
                        c.wait(y_ready, -1, 1)
                        for h in range(2):
                            c.wait(xz_done, 1, h + 3)
                            nc.scalar.activation(z_sb[:, q, h], ps_f[:, h], ACT.Identity,
                                                 bias=xz_bias[:, h + 2:h + 3]).then_inc(xz_ready, 1)
                    if front and s == 8:
                        c.wait(conv_step, 1, 2 * TAPS)
                        nc.scalar.activation(u_sb[:], u_sb[:], ACT.Silu)
                        c.wait(xz_ready, 1, 4)
                        nc.scalar.activation(z_sb[:, q], z_sb[:, q], ACT.Silu).then_inc(u_ready, 1)
                    if ffn and s == 8:
                        c.wait(lo_split, -3, BLOCKS)
                        for k in range(3):
                            c.wait(h_done, -1, k + 1)
                            nc.scalar.activation(H[:, q, k], h_bank(k), ACT.Gelu, bias=vec("b1", k)
                                                 ).then_inc(h_ready, 1)
                    if (front or ffn) and s == 8:
                        act.preload_act_table_set(EXP_LN_SET)
                    if front and s == 9:
                        c.wait(dbc_done, 1, 1)
                        nc.scalar.copy(bc_parts[0:32, q], ps_f[0:32, 0]).then_inc(hi_ready, 1)
                        nc.scalar.copy(dt_low, ps_f[64:72, 0]).then_inc(low_ready, 1)
                    if ffn and s == 9:
                        c.wait(h_done, -1, 4)
                        nc.scalar.activation(H[:, q, 3], h_bank(3), ACT.Gelu, bias=vec("b1", 3)).then_inc(h_ready, 1)
                        act.preload_act_table_set(EXP_LN_SET)
                    if front and s == 11:
                        c.wait(rest_ready, 1, 1)
                        nc.scalar.copy(bc_parts[32:64, q], bc_rest).then_inc(mid_ready, 1)
                    if front and s == 12:
                        for h in range(2):
                            c.wait(clamp_ready, 1, h + 1)
                            nc.scalar.activation(soft[:, h], soft[:, h], ACT.Exp).then_inc(exp_ready, 1)
                        for h in range(2):
                            c.wait(exp_ready, 1, h + 1)
                            nc.scalar.activation(soft[:, h], soft[:, h], ACT.Ln, bias=1.0).then_inc(soft_ready, 1)
                    if ffn and s == 13:
                        c.wait(gate_step, -1, 3)
                        nc.scalar.activation(expo[:], logit[:], ACT.Exp).then_inc(expo_ready, 1)
                    if ffn and s == 15:
                        c.wait(coef_t_done, -1, 1)
                        nc.scalar.copy(coef_t, ps_y[0:EXPERTS, 0]).then_inc(coef_t_ready, 1)
                    for d, b in next_split(s, ffn, experts):
                        c.wait(h_ready, d, 4)
                        c.wait(yexp_done, *unit_before(d, b))
                        nc.scalar.copy(H_parts[:, 0, b % 2], H[:, q if d == -1 else p, :, b * P:(b + 1) * P]
                                       ).then_inc(hi_split, 1)
                    for d, t in next_state(s, mamba, front):
                        c.wait(c_done, d, t + 1)
                        c.wait(hc_ready, d, t - 1)
                        nc.scalar.copy(c_wide[:, t % 2], ps_c[:, 0]).then_inc(c_ready, 1)
                        c.wait(dt_ready, d, 2)
                        c.wait(scan_ready, d, t - 1)
                        for h in range(2):
                            exp = nc.scalar.activation(decay[:, t % 2, h], dt_sb[:, p if d == 0 else q, h], ACT.Exp,
                                                       scale=negA[:, h, t:t + 1])
                        exp.then_inc(decay_ready, 1)

            bodies(act, body)

        @block.vector
        def _(dve):
            nc.vector.memset(state[:], 0.0).then_inc(start_v, 1)
            nc.vector.memset(conv_in[:], 0.0).then_inc(start_v, 1)
            nc.vector.memset(eps_col[:], EPS).then_inc(start_v, 1)
            quarter = J // 4
            half = quarter // 2

            def rows(ap, first):
                return ap[:, first:first + half].unsqueeze(2).broadcast_to([P, half, P])

            for e in range(8):
                first = e * half
                block_ = nodes[:, first:first + half]
                if e % 2 == 0:
                    dve.wait_ge(node_in[e // 2], 16)
                nc.vector.reduce_sum(row_sum[:, first:first + half], block_, AX).then_inc(node_sum, 1)
                dve.wait_ge(node_sum, e + 1)
                nc.vector.scalar_tensor_tensor(out=block_, in0=rows(row_sum, first), scalar=-1.0 / P, in1=block_,
                                               op0=ALU.mult, op1=ALU.add).then_inc(node_cen, 1)
                dve.wait_ge(node_sq, e + 1)
                nc.vector.reduce_sum(row_rstd[:, first:first + half], scratch(e % 2, half), AX).then_inc(node_var, 1)
                if e % 2:
                    for f in (first - half, first):
                        if f == first - half:
                            dve.wait_ge(node_rstd, e // 2 + 1)
                        nc.vector.tensor_tensor(nodes[:, f:f + half], nodes[:, f:f + half], rows(row_rstd, f),
                                                ALU.mult).then_inc(node_ready, 1)
            dve.wait_ge(weights_in, 16 * 12)
            dve.wait_ge(start_a, 1)
            nc.vector.tensor_scalar_mul(negA[:], negA[:], -1.0).then_inc(start_v, 1)
            dve.wait_ge(start_p, 1)
            nc.vector.tensor_scalar_mul(win_sb[:], win_sb[:], vec("ln_g")).then_inc(start_v, 1)
            dve.wait_ge(start_a, 3)
            nc.vector.tensor_tensor(wd_parts[:, 1], wd_sb, wd_parts[:, 0].bitcast(F32), ALU.subtract
                                    ).then_inc(start_v, 1)
            dve.wait_ge(start_v, 6)

            def body(i, p, adjacency, front, mamba, ffn, experts):
                c = Count(dve, i)
                q = 1 - p

                def combine(u):
                    b, n = u // 4, u % 4
                    if u == 0:
                        c.wait(base_ready, -2, 1)
                    c.wait(yexp_done, -2, u + 1)
                    c.wait(acc_step, -2, 9 * b + 2 * n)
                    for e in (2 * n, 2 * n + 1):
                        src = ps_e[:, n % 2, (e % 2) * P:(e % 2 + 1) * P]
                        w = coef[:, p, b, e:e + 1]
                        if e == 1:
                            step = nc.vector.tensor_scalar_mul(odd_acc[:], src, w)
                        else:
                            acc = odd_acc[:] if e % 2 else out_sb[:, p, b]
                            step = nc.vector.scalar_tensor_tensor(out=acc, in0=src, scalar=w, in1=acc,
                                                                  op0=ALU.mult, op1=ALU.add)
                        step.then_inc(acc_step, 1)
                    if n == 3:
                        c.wait(acc_step, -2, 9 * b + 8)
                        nc.vector.tensor_tensor(out_sb[:, p, b], out_sb[:, p, b], odd_acc[:], ALU.add
                                                ).then_inc(acc_step, 1)

                for s in range(SLOTS):
                    if ffn and s == 3:
                        c.wait(wout_done, -1, 1)
                        c.wait(x_in, -1, 16)
                        c.wait(base_done, -1, 0)
                        nc.vector.tensor_tensor(x1[:], ps_y[:, 0], x_tile[:], ALU.add).then_inc(x1_ready, 1)
                    if front and s == 4:
                        c.wait(rstd_ready, 1, 1)
                        nc.vector.tensor_tensor(front_a[:], ps_f[:, 0], front_b[:], ALU.mult).then_inc(hn_ready, 1)
                    if ffn and s == 6:
                        c.wait(cen2_kept, -1, 1)
                        c.wait(rstd2_ready, -1, 1)
                        nc.vector.tensor_tensor(ffn_a[:], x_tile[:], ffn_b[:], ALU.mult).then_inc(xn_ready, 1)
                    if front and s == 10:
                        c.wait(hi_ready, 1, 1)
                        c.wait(lo_ready, 1, 0)
                        nc.vector.tensor_tensor(bc_rest, ps_f[0:32, 0], bc_parts[0:32, q], ALU.subtract
                                                ).then_inc(rest_ready, 1)
                    if front and s == 11:
                        c.wait(wout_done, 0, 0)
                        for h in range(2):
                            c.wait(dt_done, 1, h + 1)
                            nc.vector.tensor_scalar(soft[:, h], ps_f[:, 1 - h], vec("b_dt", h), CLAMP,
                                                    ALU.add, ALU.min).then_inc(clamp_ready, 1)
                    if front and s == 12:
                        c.wait(mid_ready, 1, 1)
                        nc.vector.tensor_tensor(bc_parts[64:96, q], bc_rest, bc_parts[32:64, q],
                                                ALU.subtract).then_inc(lo_ready, 1)
                    if ffn and s == 12:
                        c.wait(logit_done, -1, 1)
                        c.wait(gate_step, -1, 0)
                        nc.vector.tensor_tensor(logit[:], ps_y[:, 0, 0:BLOCKS * EXPERTS].rearrange(
                            "p (b e) -> p b e", b=BLOCKS), over_blocks(vec("bg", 0, EXPERTS)), ALU.add
                            ).then_inc(gate_step, 1)
                        c.wait(gate_step, -1, 1)
                        nc.vector.reduce_max(top[:, 0], logit[:], AX).then_inc(gate_step, 1)
                        c.wait(gate_step, -1, 2)
                        nc.vector.tensor_tensor(logit[:], logit[:], over_experts(top[:, 0]), ALU.subtract
                                                ).then_inc(gate_step, 1)
                    if front and s == 13:
                        for h in range(2):
                            c.wait(soft_ready, 1, h + 1)
                            nc.vector.scalar_tensor_tensor(out=dt_sb[:, q, h], in0=ps_f[:, 1 - h],
                                                           scalar=vec("b_dt", h), in1=soft[:, h], op0=ALU.add,
                                                           op1=ALU.max).then_inc(dt_ready, 1)
                    if ffn and s == 14:
                        c.wait(gate_step, -1, 3)
                        nc.vector.scalar_tensor_tensor(out=pick[:], in0=logit[:], scalar=0.0,
                                                       in1=over_blocks(vec("desc", 0, EXPERTS)), op0=ALU.is_ge,
                                                       op1=ALU.mult).then_inc(gate_step, 1)
                        c.wait(expo_ready, -1, 1)
                        nc.vector.reduce_sum(top[:, 2], expo[:], AX).then_inc(gate_step, 1)
                        c.wait(gate_step, -1, 4)
                        nc.vector.reduce_max(top[:, 1], pick[:], AX).then_inc(gate_step, 1)
                        c.wait(gate_step, -1, 5)
                        nc.vector.reciprocal(top[:, 3], top[:, 2]).then_inc(gate_step, 1)
                        c.wait(gate_step, -1, 6)
                        nc.vector.tensor_tensor(pick[:], over_blocks(vec("desc", 0, EXPERTS)), over_experts(top[:, 1]),
                                                ALU.is_equal).then_inc(gate_step, 1)
                        c.wait(gate_step, -1, 8)
                        nc.vector.tensor_tensor(coef[:, q], pick[:], over_experts(top[:, 3]), ALU.mult
                                                ).then_inc(gate_step, 1)
                    if front and s == 15:
                        c.wait(inject_ready, 0, SLOTS)
                        c.wait(dt_ready, 1, 2)
                        c.wait(u_ready, 1, 1)
                        nc.vector.tensor_tensor(dtu_sb[:], dt_sb[:, q], u_sb[:], ALU.mult
                                                ).then_inc(dtu_ready, 1)
                    if mamba:
                        c.wait(decay_ready, 0, s + 1)
                        c.wait(inject_ready, 0, s + 1)
                        c.wait(state_ready, 0, s - 1)
                        for h in range(2):
                            scan = nc.vector.tensor_tensor_scan(hidden[:, s % 2, h], decay[:, s % 2, h],
                                                                inject[:, s % 2, h], state[:, h, s:s + 1],
                                                                ALU.mult, ALU.add)
                        scan.then_inc(scan_ready, 1)
                    for d, t in next_state(s, mamba, front):
                        c.wait(dtu_ready, d, 1)
                        c.wait(b_done, d, t + 1)
                        c.wait(scan_ready, d, t - 1)
                        nc.vector.tensor_tensor(inject[:, t % 2], dtu_sb[:],
                                                over_halves(ps_b[:, 0]), ALU.mult).then_inc(inject_ready, 1)
                    if ffn and s < 2:
                        t = SLOTS - 2 + s
                        c.wait(hc_ready, -1, t + 1)
                        c.wait(y_step, -1, t)
                        nc.vector.tensor_tensor(y_sum[:], y_sum[:], h_c[:, t % 2], ALU.add).then_inc(y_step, 1)
                    if ffn and s == 1:
                        c.wait(y_step, -1, SLOTS)
                        nc.vector.tensor_tensor(y_gated[:], y_sum[:], z_sb[:, q], ALU.mult).then_inc(y_ready, 1)
                    if mamba:
                        if s == 2:
                            c.wait(hc_ready, 0, 1)
                            c.wait(u_ready, 0, 1)
                            c.wait(y_ready, 0, 0)
                            for h in range(2):
                                step = nc.vector.scalar_tensor_tensor(
                                    out=y_sum[:, h], in0=u_sb[:, h], scalar=vec("D", h), in1=h_c[:, 0, h],
                                    op0=ALU.mult, op1=ALU.add)
                            step.then_inc(y_step, 1)
                        elif s > 2:
                            c.wait(hc_ready, 0, s - 1)
                            c.wait(y_step, 0, s - 2)
                            nc.vector.tensor_tensor(y_sum[:], y_sum[:], h_c[:, s % 2], ALU.add).then_inc(y_step, 1)
                    if experts and s:
                        combine(s - 1)
                    if experts and s == SLOTS - 1:
                        combine(s)
                    if front and s == 6:
                        c.wait(xz_ready, 1, 2)
                        for k in range(TAPS):
                            for h in range(2):
                                src = conv_in[:, h, k:k + T]
                                w = vec("conv_w", TAPS * h + k)
                                if k == 0:
                                    step = nc.vector.tensor_scalar(u_sb[:, h], src, w, vec("conv_b", h),
                                                                   ALU.mult, ALU.add)
                                else:
                                    c.wait(conv_step, 1, 2 * k + h - 1)
                                    step = nc.vector.scalar_tensor_tensor(
                                        out=u_sb[:, h], in0=src, scalar=w, in1=u_sb[:, h],
                                        op0=ALU.mult, op1=ALU.add)
                                step.then_inc(conv_step, 1)

            bodies(dve, body)

        @block.tensor
        def _(pe):
            def product(dst, pairs):
                for n, (stationary, moving) in enumerate(pairs):
                    last = nc.tensor.matmul(dst, stationary, moving, start=(n == 0), stop=(n == len(pairs) - 1))
                return last

            pe.wait_ge(weights_in, 16 * 12)
            for k in range(4):
                last = nc.tensor.matmul(ps_y[:, 0, k:k + 1], win_sb[:, k], vec("ln_b"), start=True, stop=True)
            last.then_inc(start_p, 1)
            pe.wait_ge(start_a, 2)
            pe.wait_ge(start_v, 5)

            def body(i, p, adjacency, front, mamba, ffn, experts):
                c = Count(pe, i)
                q = 1 - p
                for s in range(SLOTS):
                    for d, t in next_state(s, mamba, front):
                        c.wait(lo_ready, d, 1)
                        c.wait(c_ready, d, t)
                        nc.tensor.matmul(ps_c[:, 0], picks(SLOTS + t), bc_parts[:, p if d == 0 else q], start=True,
                                         stop=True).then_inc(c_done, 1)
                    def broadcast_b():
                        for d, t in next_state(s, mamba, front):
                            c.wait(inject_ready, d, t)
                            nc.tensor.matmul(ps_b[:, 0], picks(t), bc_parts[:, p if d == 0 else q], start=True,
                                             stop=True).then_inc(b_done, 1)

                    def unit():
                        b, n = s // 4, s % 4
                        c.wait(acc_step, -2, 9 * ((s - 2) // 4) + 2 * ((s - 2) % 4) + 2 if s >= 2 else 0)
                        if n == 0:
                            c.wait(lo_split, -2, b + 1)
                        product(ps_e[:, n % 2, 0:2 * P],
                                [(H_parts[:, h, b % 2, k],
                                  wd_parts[:, w, k, 2 * n:2 * n + 2].rearrange("p e c -> p (e c)"))
                                 for k in range(4) for h, w in ((0, 0), (0, 1), (1, 0))]).then_inc(yexp_done, 1)

                    if not adjacency:
                        broadcast_b()
                        if experts:
                            unit()
                    else:
                        for m in adj_blocks(s):
                            if m == adj_blocks(s)[len(adj_blocks(s)) // 2]:
                                broadcast_b()
                                if experts:
                                    unit()
                            g = m // GROUP
                            if m == 0:
                                c.wait(agg_ready, 2, 0)
                            if m % GROUP == 0:
                                fills = GROUPS // RING
                                pe.wait_ge(ring_in[g % RING], c.times_of(16 * fills) + (2 * fills + g // RING + 1) * 16)
                                if isinstance(i, int) and i == -2 and m % (J // 8) == 0:
                                    pe.wait_ge(node_ready, m // (J // 8) + 1)
                            last = nc.tensor.matmul(ps_adj[:, 0], nodes[:, m], ring[:, g % RING, m % GROUP],
                                                    start=(m == 0), stop=(m == J - 1))
                            if m % GROUP == GROUP - 1:
                                last.then_inc(adj_used, 1)
                    if front and s == 0:
                        c.wait(agg_ready, 1, 1)
                        c.wait(dt_ready, 1, 0)
                        product(ps_f[:, 0], [(gcn_sb[:], front_a[:])]).then_inc(gcn_done, 1)
                    if front and s == 1:
                        c.wait(gcn_ready, 1, 1)
                        product(ps_f[:, 0], [(center, front_b[:])]).then_inc(cen_done, 1)
                    if front and s == 2:
                        c.wait(sq_ready, 1, 1)
                        product(ps_f[:, 1], [(mean, front_a[:])]).then_inc(var_done, 1)
                    if ffn and s == 2:
                        c.wait(y_ready, -1, 1)
                        c.wait(base_ready, -1, 0)
                        product(ps_y[:, 0], [(wout_sb[:, h], y_gated[:, h]) for h in range(2)]
                                ).then_inc(wout_done, 1)
                    if ffn and s == 3:
                        c.wait(x1_ready, -1, 1)
                        product(ps_y[:, 0], [(center, x1[:])]).then_inc(cen2_done, 1)
                    if front and s == 4:
                        c.wait(hn_ready, 1, 1)
                        for k in range(2):
                            product(ps_f[:, k], [(win_sb[:, k], front_a[:])]).then_inc(xz_done, 1)
                    if ffn and s == 4:
                        c.wait(cen2_kept, -1, 1)
                        product(ps_y[:, 0], [(mean, ffn_a[:])]).then_inc(var2_done, 1)
                    if front and s == 5:
                        for k in range(2):
                            c.wait(xz_ready, 1, k + 1)
                            product(ps_f[:, k], [(win_sb[:, 2 + k], front_a[:])]).then_inc(xz_done, 1)
                    if ffn and s == 7:
                        c.wait(xn_ready, -1, 1)
                        c.wait(xz_ready, 1 if front else 0, 4 if front else 0)
                        for k in range(3):
                            product(h_bank(k), [(w1_sb[:, k], ffn_a[:])]).then_inc(h_done, 1)
                    if ffn and s == 8:
                        c.wait(h_ready, -1, 2)
                        product(h_bank(3), [(w1_sb[:, 3], ffn_a[:])]).then_inc(h_done, 1)
                    if front and s == 8:
                        c.wait(u_ready, 1, 1)
                        product(ps_f[0:96, 0], [(wxp_sb[:, h], u_sb[:, h]) for h in range(2)]
                                ).then_inc(dbc_done, 1)
                    if front and s == 9:
                        c.wait(low_ready, 1, 1)
                        if ffn:
                            c.wait(h_ready, -1, 4)
                        product(ps_f[:, 1], [(wdt_sb[:, 0], dt_low)]).then_inc(dt_done, 1)
                    if front and s == 10:
                        c.wait(rest_ready, 1, 1)
                        product(ps_f[:, 0], [(wdt_sb[:, 1], dt_low)]).then_inc(dt_done, 1)
                    if ffn and s == 10:
                        c.wait(h_ready, -1, 4)
                        for b in range(BLOCKS):
                            last = product(ps_y[:, 0, b * EXPERTS:(b + 1) * EXPERTS],
                                           [(H[:, q, k, b * P:(b + 1) * P], wg_sb[:, k]) for k in range(4)])
                        last.then_inc(logit_done, 1)
                    if ffn and s == 14:
                        c.wait(gate_step, -1, 9)
                        for b in range(BLOCKS):
                            last = product(ps_y[0:EXPERTS, 0, b * P:(b + 1) * P], [(coef[:, q, b], ident)])
                        last.then_inc(coef_t_done, 1)
                    if ffn and s == 15:
                        c.wait(coef_t_ready, -1, 1)
                        for b in range(BLOCKS):
                            last = product(ps_y[:, 0, b * P:(b + 1) * P],
                                           [(x1[:, b * P:(b + 1) * P], ident), (coef_t[:, b * P:(b + 1) * P], bd_sb)])
                        last.then_inc(base_done, 1)

            bodies(pe, body)


def kernel(**inputs):
    import ml_dtypes
    import numpy as np
    import concourse.bacc as bacc
    from concourse.bass_utils import run_bass_kernel_spmd

    a = {k.replace("L0_", ""): np.asarray(v) for k, v in inputs.items()}
    x, adj = a["x"], a["adj"]
    N, D = x.shape
    J = N // P

    def halves(v):
        return v.reshape(2, P, -1).transpose(1, 0, 2)

    vecs = np.zeros((P, NCOLS), np.float32)
    for name, v in (("gcn_b", a["gnn_gcn_b"][:, None]), ("ln_g", a["gnn_ln_g"][:, None]),
                    ("ln_b", a["gnn_ln_b"][:, None]), ("conv_w", halves(a["gnn_conv_w"]).reshape(P, -1)),
                    ("conv_b", a["gnn_conv_b"].reshape(2, P).T), ("b_dt", a["gnn_b_dt"].reshape(2, P).T),
                    ("D", a["gnn_D_skip"].reshape(2, P).T), ("b1", a["ffn_b1"].reshape(4, P).T),
                    ("A_log", halves(a["gnn_A_log"]).reshape(P, -1)),
                    ("bg", np.broadcast_to(a["ffn_bg"], (P, EXPERTS))),
                    ("desc", np.broadcast_to(np.arange(EXPERTS, 0, -1, dtype=np.float32), (P, EXPERTS)))):
        first, n = COLS[name]
        vecs[:, first:first + n] = v
    eye = np.eye(P, dtype=np.float32)
    mean = np.full((P, P), 1.0 / P, np.float32)
    consts = np.stack([eye, eye - mean, mean], axis=1)
    sel = np.tile(np.eye(32), (3, 1)).astype(ml_dtypes.bfloat16)
    w_xp = np.zeros((P, 2, 96), np.float32)
    xp = halves(a["gnn_w_xp"])
    w_xp[:, :, 0:32] = xp[:, :, 8:40]
    w_xp[:, :, 64:72] = xp[:, :, 0:8]

    arrays = {
        "x_rows": x.reshape(P, J, D), "x_cols": x.T,
        "adj": adj.reshape(N // T, T, P, J // GROUP, GROUP).transpose(0, 3, 2, 4, 1),
        "vecs": vecs, "consts": consts, "sel": sel, "gcn_w": a["gnn_gcn_w"],
        "w_in": a["gnn_w_in"].reshape(P, 4, P), "w_xp": w_xp, "w_dt": a["gnn_w_dt"].reshape(8, 2, P),
        "w_out": halves(a["gnn_w_out"]), "W1": a["ffn_W1"].reshape(P, 4, P),
        "Wg": a["ffn_Wg"].reshape(4, P, EXPERTS).transpose(1, 0, 2),
        "Wd": a["ffn_Wd"].reshape(EXPERTS, 4, P, P).transpose(2, 1, 0, 3), "bd": a["ffn_bd"],
    }
    arrays = {k: np.ascontiguousarray(v) for k, v in arrays.items()}
    nc = bacc.Bacc("TRN2", target_bir_lowering=False, num_devices=1)
    args = [nc.dram_tensor(k, v.shape, mybir.dt.from_np(v.dtype), kind="ExternalInput").ap()
            for k, v in arrays.items()]
    out = nc.dram_tensor("out", (N, D), F32, kind="ExternalOutput").ap()
    gnn_mamba_moe(nc, *args, out)
    r = run_bass_kernel_spmd(nc, [arrays], core_ids=[0])
    return r.results[0]["out"]
```

```python
from contextlib import ExitStack

import concourse.bass as bass
from concourse import mybir

P = 128
T = 512
SLOTS = 16
GROUP = 2
RING = 4
EPS = 1e-5
CLAMP = 40.0
TAPS = 4
EXPERTS = 8

ALU = mybir.AluOpType
ACT = mybir.ActivationFunctionType
F32 = mybir.dt.float32
F32R = mybir.dt.float32r
BF16 = mybir.dt.bfloat16
AX = mybir.AxisListType.X
EXP_LN_SET = "natural_log_exp_and_others"

COLS = {}
_at = 0
for _name, _n in (("gcn_b", 1), ("ln_g", 1), ("ln_b", 1), ("conv_w", 2 * TAPS), ("conv_b", 2), ("b_dt", 2),
                  ("D", 2), ("b1", 4), ("A_log", 32), ("bg", EXPERTS), ("desc", EXPERTS)):
    COLS[_name] = (_at, _n)
    _at += _n
NCOLS = _at


def gnn_mamba_moe(nc, x_rows, x_cols, adj, vecs, consts, sel, gcn_w, w_in, w_xp, w_dt, w_out, W1, Wg, Wd, bd, out):
    J = x_rows.shape[1]
    N = x_cols.shape[1]
    TILES = N // T
    GROUPS = J // GROUP
    BLOCKS = T // P
    UNITS = BLOCKS * EXPERTS // 4
    assert TILES % 2 == 0 and TILES >= 6 and GROUPS % RING == 0 and GROUP * GROUPS == J

    with ExitStack() as ctx:
        def sb(name, shape, dt=F32):
            return ctx.enter_context(nc.sbuf_tensor(name, shape, dt))

        def bank(name, n=1):
            return ctx.enter_context(nc.psum_tensor(name, [P, n, T], F32))

        vec_sb = sb("vec_sb", [P, NCOLS])
        const_sb = sb("const_sb", [P, 3, P])
        ident, center, mean = const_sb[:, 0, :], const_sb[:, 1, :], const_sb[:, 2, :]
        sel_sb = sb("sel_sb", [96, 32], BF16)
        gcn_sb = sb("gcn_sb", [P, P])
        win_parts = sb("win_parts", [P, 2, 4, P], F32R)
        w1_parts = sb("w1_parts", [P, 2, 4, P], F32R)
        wd_parts = sb("wd_parts", [P, 2, 4, EXPERTS, P], F32R)
        wxp_sb = sb("wxp_sb", [P, 2, P])
        bd_parts = sb("bd_parts", [96, BLOCKS, P], F32R)
        wdt_parts = sb("wdt_parts", [72, 2, P], F32R)
        wout_sb = sb("wout_sb", [P, 2, P])
        wg_sb = sb("wg_sb", [P, 4, EXPERTS])
        negA = sb("negA", [P, 2, SLOTS])
        xz_bias = sb("xz_bias", [P, 4])
        eps_col = sb("eps_col", [P, 1])

        nodes = sb("nodes", [P, J, P])
        ring = sb("ring", [P, RING, GROUP, T])

        front_a = sb("front_a", [P, T])
        front_b = sb("front_b", [P, T])
        conv_in = sb("conv_in", [P, 2, TAPS - 1 + T])
        z_sb = sb("z_sb", [P, 2, 2, T])
        u_sb = sb("u_sb", [P, 2, T])
        soft = sb("soft", [P, 2, T])
        dt_sb = sb("dt_sb", [P, 2, 2, T])
        dtu_sb = sb("dtu_sb", [P, 2, T])
        low_parts = sb("low_parts", [96, T], F32R)
        coef_t = low_parts[:, 0:P]
        rows_sb = sb("rows_sb", [72, T])
        bc_rest, low_raw = rows_sb[32:64, :], rows_sb[64:72, :]
        bc_parts = sb("bc_parts", [96, 2, T], BF16)

        decay = sb("decay", [P, 2, 2, T])
        inject = sb("inject", [P, 2, T])
        hidden = sb("hidden", [P, 2, 2, T])
        c_wide = sb("c_wide", [P, 2, T])
        h_c = sb("h_c", [P, 2, 2, T])
        state = sb("state", [P, 2, SLOTS])
        y_sum = sb("y_sum", [P, 2, T])
        y_gated = soft

        x_tile = sb("x_tile", [P, T])
        x1 = sb("x1", [P, T])
        ffn_a = soft[:, 0]
        ffn_b = front_b
        H = sb("H", [P, 4, T])
        H_parts = sb("H_parts", [P, 2, 3, 4, P], F32R)
        logit = sb("logit", [P, BLOCKS, EXPERTS])
        pick = sb("pick", [P, BLOCKS, EXPERTS])
        expo = sb("expo", [P, BLOCKS, EXPERTS])
        coef = sb("coef", [P, 2, BLOCKS, EXPERTS])
        coef_parts = sb("coef_parts", [P, 3, BLOCKS, EXPERTS], F32R)
        top = sb("top", [P, 4, BLOCKS])
        out_sb = sb("out_sb", [P, 2, BLOCKS, P])
        odd_acc = sb("odd_acc", [P, P])
        norm_hi = sb("norm_hi", [P, T], F32R)
        norm_lo = sb("norm_lo", [P, T], F32R)
        wd_halves = [ap[:].rearrange("p a b n -> p (a b n)").rearrange("p (k e c) -> p k e c", k=2, e=EXPERTS)
                     for ap in (decay, dt_sb)]
        bd_sb = soft[0:96, 1].rearrange("p (b c) -> p b c", b=BLOCKS)
        wdt_sb = x1[0:72, 0:2 * P].rearrange("p (h c) -> p h c", h=2)
        win_sb, w1_sb = (u_sb[:, h].rearrange("p (k c) -> p k c", k=4) for h in range(2))
        row_sum, row_rstd = odd_acc[:, 0:J], odd_acc[:, J:2 * J]

        ps_adj = bank("ps_adj")
        ps_b = bank("ps_b")
        ps_c = bank("ps_c")
        ps_f = bank("ps_f", 2)
        ps_y = bank("ps_y")
        ps_e = bank("ps_e", 2)

        def vec(name, j=0, n=1):
            first = COLS[name][0] + j
            return vec_sb[:, first:first + n]

        def scratch(e, n):
            return (hidden, h_c)[e].rearrange("p a b n -> p (a b n)")[:, 0:n * P].rearrange("p (j d) -> p j d", d=P)

        def h_bank(k):
            return (ps_f[:, 0], ps_f[:, 1], ps_y[:, 0], ps_y[:, 0])[k]

        def picks(row):
            return sel_sb[:, row:row + 1].broadcast_to([96, P])

        def over_halves(ap):
            return ap.unsqueeze(1).broadcast_to([P, 2, T])

        def over_experts(ap):
            return ap.unsqueeze(2).broadcast_to([P, BLOCKS, EXPERTS])

        def over_blocks(ap):
            return ap.unsqueeze(1).broadcast_to([P, BLOCKS, EXPERTS])

        PER = {}

        def sem(name, per=1):
            s = ctx.enter_context(nc.semaphore(name))
            PER[name] = per
            return s

        weights_in = sem("weights_in")
        node_in = [sem(f"node_in{n}") for n in range(8)]
        ring_in = [sem(f"ring_in{r}") for r in range(RING)]
        adj_used = sem("adj_used", GROUPS)
        start_v, start_a, start_p = sem("start_v"), sem("start_a"), sem("start_p")
        node_sum, node_cen, node_sq, node_var, node_ready = (
            sem("node_sum"), sem("node_cen"), sem("node_sq"), sem("node_var"), sem("node_ready"))
        node_ln, node_rstd = sem("node_ln"), sem("node_rstd")

        agg_ready, gcn_done, gcn_ready = sem("agg_ready"), sem("gcn_done"), sem("gcn_ready")
        cen_done, sq_ready, var_done = sem("cen_done"), sem("sq_ready"), sem("var_done")
        ln_ready, rstd_ready, hn_ready = sem("ln_ready"), sem("rstd_ready"), sem("hn_ready")
        front_hi, front_lo, ffn_hi, ffn_lo = sem("front_hi"), sem("front_lo"), sem("ffn_hi"), sem("ffn_lo")
        xz_done, xz_ready, tail_ready = sem("xz_done", 4), sem("xz_ready", 4), sem("tail_ready")
        conv_first, conv_step = sem("conv_first", 2), sem("conv_step", 2 * (TAPS - 1))
        u_ready, dbc_done = sem("u_ready"), sem("dbc_done")
        hi_ready, low_ready, rest_ready, mid_ready, lo_ready = (
            sem("hi_ready"), sem("low_ready"), sem("rest_ready"), sem("mid_ready"), sem("lo_ready"))
        dt_done, clamp_ready, exp_ready, soft_ready, dt_ready, dtu_ready = (
            sem("dt_done", 2), sem("clamp_ready", 2), sem("exp_ready", 2), sem("soft_ready", 2),
            sem("dt_ready", 2), sem("dtu_ready"))

        b_done, c_done, c_ready = sem("b_done", SLOTS), sem("c_done", SLOTS), sem("c_ready", SLOTS)
        decay_ready, inject_ready, scan_ready = (
            sem("decay_ready", SLOTS), sem("inject_ready", SLOTS), sem("scan_ready", SLOTS))
        hc_ready, state_ready, y_step = sem("hc_ready", SLOTS), sem("state_ready", SLOTS), sem("y_step", SLOTS)

        y_ready, wout_done, x_in, x1_ready = sem("y_ready"), sem("wout_done"), sem("x_in", 16), sem("x1_ready")
        cen2_done, sq2_ready, var2_done = sem("cen2_done"), sem("sq2_ready"), sem("var2_done")
        ln2_ready, rstd2_ready, xn_ready = sem("ln2_ready"), sem("rstd2_ready"), sem("xn_ready")
        h_done, h_ready, logit_done = sem("h_done", 4), sem("h_ready", 4), sem("logit_done")
        gate_step = sem("gate_step", 12)
        expo_ready, coef_t_done, coef_t_ready = sem("expo_ready"), sem("coef_t_done"), sem("coef_t_ready")
        base_done, base_ready = sem("base_done"), sem("base_ready")
        low_split = sem("low_split")
        hi_split, lo_split = sem("hi_split", BLOCKS), sem("lo_split", BLOCKS)
        yexp_done, acc_step = sem("yexp_done", UNITS), sem("acc_step", 9 * BLOCKS)
        out_done = [sem("out_done_even", 8), sem("out_done_odd", 8)]
        cen2_kept = sem("cen2_kept")

        class Count:

            def __init__(self, eng, i):
                self.eng, self.i, self.times = eng, i, {}

            def times_of(self, per):
                if isinstance(self.i, int) or per == 1:
                    return self.i * per
                if per not in self.times:
                    self.times[per] = self.eng.snap(self.i * per)
                return self.times[per]

            def value(self, s, d, n):
                v = self.times_of(PER[s.name]) + (d * PER[s.name] + n)
                if isinstance(v, int):
                    return v if v > 0 else None
                return self.eng.lower_val(v)

            def wait(self, s, d, n):
                per = PER[s.name]
                v = self.times_of(per) + (d * per + n)
                if not isinstance(v, int) or v > 0:
                    self.eng.wait_ge(s, v)

        def stages(i):
            live = lambda k: 0 <= k < TILES
            return dict(adjacency=live(i + 2), front=live(i + 1), mamba=live(i), ffn=live(i - 1), experts=live(i - 2))

        ALL = dict(adjacency=True, front=True, mamba=True, ffn=True, experts=True)

        def bodies(eng, body):
            for i in range(-2, 4):
                body(i, i % 2, **stages(i))
            with eng.Fori(4, TILES - 3, 2) as i:
                body(i, 0, **ALL)
                body(i + 1, 1, **ALL)
            for i in range(TILES - 2, TILES + 2):
                body(i, i % 2, **stages(i))

        def adj_blocks(s):
            return range(J * s // SLOTS, J * (s + 1) // SLOTS)

        def next_state(s, mamba, front):
            if s + 1 < SLOTS:
                return ((0, s + 1),) if mamba else ()
            return ((1, 0),) if front else ()

        def in_tail(tile):
            return isinstance(tile, int) and tile >= TILES - 2

        def b_bank(tile, t):
            return ps_adj[:, 0] if in_tail(tile) and t % 2 else ps_b[:, 0]

        def next_split(s, ffn, experts):
            if s == 14:
                return ((-1, 0),) if ffn else ()
            return ((-2, {1: 1, 4: 2, 6: 3}[s]),) if experts and s in (1, 4, 6) else ()

        def split_buffer(parity, b):
            return ((0, 1, 2, 0), (1, 2, 0, 1))[parity][b]

        def unit_before(d, parity, b):
            if b == 3:
                return (d, 2)
            return (d - 1, ((6, 8, 4), (4, 6, 8))[parity][b])

        block = ctx.enter_context(nc.Block())

        @block.sync
        def _(sp):
            def store(c, i, q):
                summed = c.value(acc_step, -3, 9 * BLOCKS)
                sp.dma_start(out[bass.ds((i - 3) * T, T), :].rearrange("(b p) c -> p b c", p=P), out_sb[:, q]
                             ).wait_op(acc_step, summed, "sem-ge").then_inc(out_done[q], 16)

            def small_weights():
                for dst, src in ((vec_sb, vecs), (const_sb, consts), (sel_sb, sel), (gcn_sb, gcn_w), (win_sb, w_in),
                                 (wxp_sb, w_xp), (wdt_sb, w_dt), (wout_sb, w_out), (w1_sb, W1), (wg_sb, Wg),
                                 (bd_sb, bd)):
                    sp.dma_start(dst if isinstance(dst, bass.AP) else dst[:], src).then_inc(weights_in, 16)

            def body(i, p, adjacency, front, mamba, ffn, experts):
                c = Count(sp, i)
                for g in range(GROUPS):
                    if adjacency:
                        src = adj[bass.ds(i + 2, 1), g].rearrange("a p c n -> p (a c) n")
                        used = c.value(adj_used, 2, g - RING + 1)
                        dma = sp.dma_start(ring[:, g % RING], src)
                        if used is not None:
                            dma.wait_op(adj_used, used, "sem-ge")
                        dma.then_inc(ring_in[g % RING], 16)
                        if isinstance(i, int) and i == -2 and g == RING - 1:
                            small_weights()
                    if g == GROUPS // 2 and (not isinstance(i, int) or 0 <= i - 3 < TILES):
                        store(c, i, 1 - p)
                    if g == GROUPS - 2 and mamba:
                        used = c.value(xn_ready, 0, 0)
                        dma = sp.dma_start(x_tile[:], x_cols[:, bass.ds(i * T, T)])
                        if used is not None:
                            dma.wait_op(xn_ready, used, "sem-ge")
                        dma.then_inc(x_in, 16)

            bodies(sp, body)
            store(Count(sp, TILES + 2), TILES + 2, 1)
            for q in range(2):
                sp.wait_ge(out_done[q], 16 * TILES // 2)

        @block.gpsimd
        def _(pool):
            def body(i, p, adjacency, front, mamba, ffn, experts):
                c = Count(pool, i)
                q = 1 - p
                for s in range(SLOTS):
                    if front and s == 5:
                        c.wait(front_hi, 1, 1)
                        nc.gpsimd.tensor_tensor(norm_lo[:], front_a[:], norm_hi[:].bitcast(F32),
                                                ALU.subtract).then_inc(front_lo, 1)
                    if ffn and s == 7:
                        c.wait(ffn_hi, -1, 1)
                        nc.gpsimd.tensor_tensor(norm_lo[:], ffn_a, norm_hi[:].bitcast(F32),
                                                ALU.subtract).then_inc(ffn_lo, 1)
                    if front and s == 9:
                        if mamba:
                            c.wait(state_ready, 0, s)
                        c.wait(low_ready, 1, 1)
                        nc.gpsimd.tensor_tensor(low_parts[64:72], low_raw, low_parts[64:72].bitcast(F32),
                                                ALU.subtract).then_inc(low_split, 1)
                        c.wait(low_split, 1, 1)
                    for d, b in next_split(s, ffn, experts):
                        c.wait(hi_split, d, b + 1)
                        place = split_buffer(q if d == -1 else p, b)
                        nc.gpsimd.tensor_tensor(H_parts[:, 1, place], H[:, :, b * P:(b + 1) * P],
                                                H_parts[:, 0, place].bitcast(F32), ALU.subtract
                                                ).then_inc(lo_split, 1)
                    if not mamba:
                        continue
                    c.wait(scan_ready, 0, s + 1)
                    c.wait(c_ready, 0, s + 1)
                    c.wait(y_step, 0, s - 1)
                    nc.gpsimd.tensor_tensor(h_c[:, s % 2], hidden[:, s % 2], over_halves(c_wide[:, s % 2]),
                                            ALU.mult).then_inc(hc_ready, 1)
                    nc.gpsimd.tensor_copy(state[:, :, s:s + 1],
                                          hidden[:, s % 2, :, T - 1:T]).then_inc(state_ready, 1)

            bodies(pool, body)

        @block.scalar
        def _(act):
            part = J // 8
            for e in range(8):
                rows = slice(e * part, (e + 1) * part)
                act.dma_start(nodes[:, rows], x_rows[:, rows]).then_inc(node_in[e], 16)
            for h in range(2):
                act.dma_start(wd_halves[h], Wd[:, 2 * h:2 * h + 2]).then_inc(weights_in, 16)
            act.preload_act_table_set(EXP_LN_SET)
            for e in range(9):
                if e < 8:
                    act.wait_ge(node_cen, e + 1)
                    if e >= 2:
                        act.wait_ge(node_var, e - 1)
                    nc.scalar.activation(scratch(e % 2, part), nodes[:, e * part:(e + 1) * part],
                                         ACT.Square).then_inc(node_sq, 1)
                if e:
                    act.wait_ge(node_var, e)
                    rstd = row_rstd[:, (e - 1) * part:e * part]
                    nc.scalar.activation(rstd, rstd, ACT.Ln, bias=eps_col[:, 0:1], scale=1.0 / P).then_inc(node_ln, 1)
                    act.wait_ge(node_ln, e)
                    nc.scalar.activation(rstd, rstd, ACT.Exp, scale=-0.5).then_inc(node_rstd, 1)
            act.wait_ge(weights_in, 16 * 13)
            nc.scalar.activation(negA[:].rearrange("p a b -> p (a b)"), vec("A_log", 0, 32), ACT.Exp
                                 ).then_inc(start_a, 1)
            nc.scalar.copy(w1_parts[:, 0], w1_sb).then_inc(start_a, 1)
            nc.scalar.copy(wdt_parts[:], wdt_sb)
            nc.scalar.copy(bd_parts[:], bd_sb)
            for h in range(2):
                wd_copy = nc.scalar.copy(wd_parts[:, 0, 2 * h:2 * h + 2], wd_halves[h])
            wd_copy.then_inc(start_a, 1)
            act.wait_ge(start_p, 1)
            nc.scalar.copy(xz_bias[:], ps_y[:, 0, 0:4]).then_inc(start_a, 1)
            act.wait_ge(start_v, 5)
            nc.scalar.copy(win_parts[:, 0], win_sb).then_inc(start_a, 1)
            act.wait_ge(start_a, 5)

            def body(i, p, adjacency, front, mamba, ffn, experts):
                c = Count(act, i)
                q = 1 - p

                def copy_c(s):
                    for d, t in next_state(s, mamba, front):
                        c.wait(c_done, d, t + 1)
                        c.wait(hc_ready, d, t - 1)
                        nc.scalar.copy(c_wide[:, t % 2], ps_c[:, 0]).then_inc(c_ready, 1)

                def exp_decay(s):
                    for d, t in next_state(s, mamba, front):
                        c.wait(dt_ready, d, 2)
                        c.wait(scan_ready, d, t - 1)
                        for h in range(2):
                            exp = nc.scalar.activation(decay[:, t % 2, h], dt_sb[:, p if d == 0 else q, h], ACT.Exp,
                                                       scale=negA[:, h, t:t + 1])
                        exp.then_inc(decay_ready, 1)

                for s in range(SLOTS):
                    if front and s == 0:
                        c.wait(adj_used, 1, GROUPS)
                        c.wait(xz_done, 1, 0)
                        nc.scalar.copy(front_a[:], ps_adj[:, 0]).then_inc(agg_ready, 1)
                    if experts and s == 0:
                        c.wait(base_done, -2, 1)
                        c.wait(out_done[p], 0, -16 - 8 * p)
                        nc.scalar.copy(out_sb[:, p].rearrange("p b c -> p (b c)"), ps_y[:, 0]).then_inc(base_ready, 1)
                    if front and s == 1:
                        c.wait(gcn_done, 1, 1)
                        nc.scalar.activation(front_b[:], ps_f[:, 0], ACT.Relu, bias=vec("gcn_b")
                                             ).then_inc(gcn_ready, 1)
                    if front and s == 2:
                        c.wait(cen_done, 1, 1)
                        nc.scalar.activation(front_a[:], ps_f[:, 0], ACT.Square).then_inc(sq_ready, 1)
                    if front and s == 3:
                        c.wait(var_done, 1, 1)
                        nc.scalar.activation(front_b[:], ps_f[:, 1], ACT.Ln, bias=eps_col[:, 0:1]).then_inc(ln_ready, 1)
                        c.wait(ln_ready, 1, 1)
                        nc.scalar.activation(front_b[:], front_b[:], ACT.Exp, scale=-0.5).then_inc(rstd_ready, 1)
                    if ffn and s == 4:
                        c.wait(cen2_done, -1, 1)
                        nc.scalar.activation(ffn_a, ps_y[:, 0], ACT.Square).then_inc(sq2_ready, 1)
                        nc.scalar.copy(x_tile[:], ps_y[:, 0]).then_inc(cen2_kept, 1)
                    if ffn and s == 5:
                        c.wait(var2_done, -1, 1)
                        if front:
                            c.wait(hn_ready, 1, 1)
                        nc.scalar.activation(ffn_b[:], ps_y[:, 0], ACT.Ln, bias=eps_col[:, 0:1]).then_inc(ln2_ready, 1)
                        c.wait(ln2_ready, -1, 1)
                        nc.scalar.activation(ffn_b[:], ffn_b[:], ACT.Exp, scale=-0.5).then_inc(rstd2_ready, 1)
                    if front and s == 5:
                        c.wait(hn_ready, 1, 1)
                        c.wait(h_done, -1, 0)
                        nc.scalar.copy(norm_hi[:], front_a[:]).then_inc(front_hi, 1)
                    if front and s == 6:
                        c.wait(conv_step, 1, 0)
                        nc.scalar.copy(conv_in[:, :, 0:TAPS - 1], conv_in[:, :, T:T + TAPS - 1]
                                       ).then_inc(tail_ready, 1)
                        c.wait(tail_ready, 1, 1)
                        for h in range(2):
                            c.wait(xz_done, 1, h + 1)
                            nc.scalar.activation(conv_in[:, h, TAPS - 1:], ps_f[:, h], ACT.Identity,
                                                 bias=xz_bias[:, h:h + 1]).then_inc(xz_ready, 1)
                    if front and s == 7:
                        c.wait(y_step, 0, 1)
                        for h in range(2):
                            c.wait(xz_ready, 1, h + 1)
                            nc.scalar.activation(u_sb[:, h], conv_in[:, h, 0:T], ACT.Identity,
                                                 bias=vec("conv_b", h), scale=vec("conv_w", TAPS * h)
                                                 ).then_inc(conv_first, 1)
                    if ffn and s == 7:
                        c.wait(xn_ready, -1, 1)
                        if front:
                            c.wait(xz_done, 1, 4)
                        nc.scalar.copy(norm_hi[:], ffn_a).then_inc(ffn_hi, 1)
                    if front and s == 7:
                        c.wait(y_ready, -1, 1)
                        for h in range(2):
                            c.wait(xz_done, 1, h + 3)
                            nc.scalar.activation(z_sb[:, q, h], ps_f[:, h], ACT.Identity,
                                                 bias=xz_bias[:, h + 2:h + 3]).then_inc(xz_ready, 1)
                    if s == 8:
                        exp_decay(s)
                    if s == 10:
                        copy_c(s)
                    if front and s == 8:
                        c.wait(xz_ready, 1, 4)
                        nc.scalar.activation(z_sb[:, q], z_sb[:, q], ACT.Silu)
                        c.wait(conv_step, 1, 2 * (TAPS - 1))
                        nc.scalar.activation(u_sb[:], u_sb[:], ACT.Silu).then_inc(u_ready, 1)
                    if s == 8:
                        copy_c(s)
                    if ffn and s == 8:
                        c.wait(lo_split, -2, BLOCKS)
                        for k in range(3):
                            c.wait(h_done, -1, k + 1)
                            nc.scalar.activation(H[:, k], h_bank(k), ACT.Gelu, bias=vec("b1", k)
                                                 ).then_inc(h_ready, 1)
                    if (front or ffn) and s == 8:
                        act.preload_act_table_set(EXP_LN_SET)
                    if front and s == 9:
                        c.wait(dbc_done, 1, 1)
                        nc.scalar.copy(bc_parts[0:32, q], ps_f[96:128, 0]).then_inc(hi_ready, 1)
                        c.wait(dt_done, 1, 0)
                        nc.scalar.copy(low_parts[0:72], ps_f[0:72, 0])
                        nc.scalar.copy(low_raw, ps_f[64:72, 0]).then_inc(low_ready, 1)
                    if front and s == 11:
                        c.wait(rest_ready, 1, 1)
                        nc.scalar.copy(bc_parts[32:64, q], bc_rest).then_inc(mid_ready, 1)
                    if front and s == 12:
                        for h in range(2):
                            c.wait(clamp_ready, 1, h + 1)
                            nc.scalar.activation(soft[:, h], soft[:, h], ACT.Exp).then_inc(exp_ready, 1)
                        for h in range(2):
                            c.wait(exp_ready, 1, h + 1)
                            nc.scalar.activation(soft[:, h], soft[:, h], ACT.Ln, bias=1.0).then_inc(soft_ready, 1)
                    if ffn and s == 13:
                        c.wait(gate_step, -1, 3)
                        nc.scalar.activation(expo[:], logit[:], ACT.Exp).then_inc(expo_ready, 1)
                    if ffn and s == 15:
                        c.wait(coef_t_done, -1, 1)
                        nc.scalar.copy(coef_t, ps_y[0:96, 0, 0:P]).then_inc(coef_t_ready, 1)
                    for d, b in next_split(s, ffn, experts):
                        c.wait(h_ready, d, 4)
                        parity = q if d == -1 else p
                        c.wait(yexp_done, *unit_before(d, parity, b))
                        nc.scalar.copy(H_parts[:, 0, split_buffer(parity, b)], H[:, :, b * P:(b + 1) * P]
                                       ).then_inc(hi_split, 1)
                    if s not in (8, 10):
                        copy_c(s)
                    if s != 8:
                        exp_decay(s)
                    if ffn and s == 10:
                        c.wait(h_done, -1, 4)
                        nc.scalar.activation(H[:, 3], h_bank(3), ACT.Gelu, bias=vec("b1", 3)).then_inc(h_ready, 1)
                        act.preload_act_table_set(EXP_LN_SET)

            bodies(act, body)

        @block.vector
        def _(dve):
            nc.vector.memset(state[:], 0.0).then_inc(start_v, 1)
            nc.vector.memset(conv_in[:], 0.0).then_inc(start_v, 1)
            nc.vector.memset(eps_col[:], EPS).then_inc(start_v, 1)
            part = J // 8

            def rows(ap, e):
                return ap[:, e * part:(e + 1) * part].unsqueeze(2).broadcast_to([P, part, P])

            for e in range(10):
                if e < 8:
                    block_ = nodes[:, e * part:(e + 1) * part]
                    dve.wait_ge(node_in[e], 16)
                    nc.vector.reduce_sum(row_sum[:, e * part:(e + 1) * part], block_, AX).then_inc(node_sum, 1)
                    dve.wait_ge(node_sum, e + 1)
                    nc.vector.scalar_tensor_tensor(out=block_, in0=rows(row_sum, e), scalar=-1.0 / P, in1=block_,
                                                   op0=ALU.mult, op1=ALU.add).then_inc(node_cen, 1)
                if 1 <= e < 9:
                    dve.wait_ge(node_sq, e)
                    nc.vector.reduce_sum(row_rstd[:, (e - 1) * part:e * part], scratch((e - 1) % 2, part), AX
                                         ).then_inc(node_var, 1)
                if e >= 2:
                    block_ = nodes[:, (e - 2) * part:(e - 1) * part]
                    dve.wait_ge(node_rstd, e - 1)
                    nc.vector.tensor_tensor(block_, block_, rows(row_rstd, e - 2), ALU.mult).then_inc(node_ready, 1)
            dve.wait_ge(weights_in, 16 * 13)
            dve.wait_ge(start_a, 1)
            nc.vector.tensor_scalar_mul(negA[:], negA[:], -1.0).then_inc(start_v, 1)
            dve.wait_ge(start_p, 1)
            nc.vector.tensor_scalar_mul(win_sb, win_sb, vec("ln_g")).then_inc(start_v, 1)
            dve.wait_ge(start_a, 3)
            nc.vector.tensor_tensor(w1_parts[:, 1], w1_sb, w1_parts[:, 0].bitcast(F32), ALU.subtract
                                    ).then_inc(start_v, 1)
            nc.vector.tensor_tensor(wdt_parts[32:40], wdt_sb[32:40], wdt_parts[32:40].bitcast(F32), ALU.subtract
                                    ).then_inc(start_v, 1)
            nc.vector.tensor_tensor(bd_parts[32:64], bd_sb[32:64], bd_parts[32:64].bitcast(F32), ALU.subtract
                                    ).then_inc(start_v, 1)
            for h in range(2):
                nc.vector.tensor_tensor(wd_parts[:, 1, 2 * h:2 * h + 2], wd_halves[h],
                                        wd_parts[:, 0, 2 * h:2 * h + 2].bitcast(F32), ALU.subtract
                                        ).then_inc(start_v, 1)
            dve.wait_ge(start_a, 5)
            nc.vector.tensor_tensor(win_parts[:, 1], win_sb, win_parts[:, 0].bitcast(F32), ALU.subtract
                                    ).then_inc(start_v, 1)
            dve.wait_ge(start_v, 11)

            def body(i, p, adjacency, front, mamba, ffn, experts):
                c = Count(dve, i)
                q = 1 - p

                def combine(v):
                    b, n = v // 4, v % 4
                    if v == 0:
                        c.wait(base_ready, -2, 1)
                    c.wait(yexp_done, -2, v // 2 + 1)
                    c.wait(acc_step, -2, 9 * b + 2 * n)
                    for e in (2 * n, 2 * n + 1):
                        src = ps_e[:, v // 2 % 2, (e % 4) * P:(e % 4 + 1) * P]
                        w = coef[:, p, b, e:e + 1]
                        if e == 1:
                            step = nc.vector.tensor_scalar_mul(odd_acc[:], src, w)
                        else:
                            acc = odd_acc[:] if e % 2 else out_sb[:, p, b]
                            step = nc.vector.scalar_tensor_tensor(out=acc, in0=src, scalar=w, in1=acc,
                                                                  op0=ALU.mult, op1=ALU.add)
                        step.then_inc(acc_step, 1)
                    if n == 3:
                        c.wait(acc_step, -2, 9 * b + 8)
                        nc.vector.tensor_tensor(out_sb[:, p, b], out_sb[:, p, b], odd_acc[:], ALU.add
                                                ).then_inc(acc_step, 1)

                for s in range(SLOTS):
                    if ffn and s == 3:
                        c.wait(wout_done, -1, 1)
                        c.wait(x_in, -1, 16)
                        c.wait(base_done, -1, 0)
                        nc.vector.tensor_tensor(x1[:], ps_y[:, 0], x_tile[:], ALU.add).then_inc(x1_ready, 1)
                    if front and s == 4:
                        c.wait(rstd_ready, 1, 1)
                        nc.vector.tensor_tensor(front_a[:], ps_f[:, 0], front_b[:], ALU.mult).then_inc(hn_ready, 1)
                    if ffn and s == 6:
                        c.wait(cen2_kept, -1, 1)
                        c.wait(rstd2_ready, -1, 1)
                        nc.vector.tensor_tensor(ffn_a, x_tile[:], ffn_b[:], ALU.mult).then_inc(xn_ready, 1)
                    if front and s == 10:
                        c.wait(hi_ready, 1, 1)
                        c.wait(lo_ready, 1, 0)
                        nc.vector.tensor_tensor(bc_rest, ps_f[96:128, 0], bc_parts[0:32, q], ALU.subtract
                                                ).then_inc(rest_ready, 1)
                    if front and s == 11:
                        c.wait(wout_done, 0, 0)
                        for h in range(2):
                            c.wait(dt_done, 1, h + 1)
                            nc.vector.tensor_scalar(soft[:, h], ps_f[:, 1 - h], vec("b_dt", h), CLAMP,
                                                    ALU.add, ALU.min).then_inc(clamp_ready, 1)
                    if front and s == 12:
                        c.wait(mid_ready, 1, 1)
                        nc.vector.tensor_tensor(bc_parts[64:96, q], bc_rest, bc_parts[32:64, q],
                                                ALU.subtract).then_inc(lo_ready, 1)
                    if ffn and s == 12:
                        c.wait(logit_done, -1, 1)
                        c.wait(gate_step, -1, 0)
                        nc.vector.tensor_tensor(logit[:], ps_y[:, 0, 0:BLOCKS * EXPERTS].rearrange(
                            "p (b e) -> p b e", b=BLOCKS), over_blocks(vec("bg", 0, EXPERTS)), ALU.add
                            ).then_inc(gate_step, 1)
                        c.wait(gate_step, -1, 1)
                        nc.vector.reduce_max(top[:, 0], logit[:], AX).then_inc(gate_step, 1)
                        c.wait(gate_step, -1, 2)
                        nc.vector.tensor_tensor(logit[:], logit[:], over_experts(top[:, 0]), ALU.subtract
                                                ).then_inc(gate_step, 1)
                    if front and s == 13:
                        for h in range(2):
                            c.wait(soft_ready, 1, h + 1)
                            nc.vector.scalar_tensor_tensor(out=dt_sb[:, q, h], in0=ps_f[:, 1 - h],
                                                           scalar=vec("b_dt", h), in1=soft[:, h], op0=ALU.add,
                                                           op1=ALU.max).then_inc(dt_ready, 1)
                    if ffn and s == 14:
                        c.wait(gate_step, -1, 3)
                        nc.vector.scalar_tensor_tensor(out=pick[:], in0=logit[:], scalar=0.0,
                                                       in1=over_blocks(vec("desc", 0, EXPERTS)), op0=ALU.is_ge,
                                                       op1=ALU.mult).then_inc(gate_step, 1)
                        c.wait(expo_ready, -1, 1)
                        nc.vector.reduce_sum(top[:, 2], expo[:], AX).then_inc(gate_step, 1)
                        c.wait(gate_step, -1, 4)
                        nc.vector.reduce_max(top[:, 1], pick[:], AX).then_inc(gate_step, 1)
                        c.wait(gate_step, -1, 5)
                        nc.vector.reciprocal(top[:, 3], top[:, 2]).then_inc(gate_step, 1)
                        c.wait(gate_step, -1, 6)
                        nc.vector.tensor_tensor(pick[:], over_blocks(vec("desc", 0, EXPERTS)), over_experts(top[:, 1]),
                                                ALU.is_equal).then_inc(gate_step, 1)
                        c.wait(gate_step, -1, 8)
                        nc.vector.tensor_tensor(coef[:, q], pick[:], over_experts(top[:, 3]), ALU.mult
                                                ).then_inc(gate_step, 1)
                        c.wait(gate_step, -1, 9)
                        for part in range(2):
                            nc.vector.tensor_copy(coef_parts[:, part], coef[:, q]).then_inc(gate_step, 1)
                        c.wait(gate_step, -1, 11)
                        nc.vector.tensor_tensor(coef_parts[:, 2], coef[:, q], coef_parts[:, 0].bitcast(F32),
                                                ALU.subtract).then_inc(gate_step, 1)
                    if front and s == 15:
                        c.wait(inject_ready, 0, SLOTS)
                        c.wait(dt_ready, 1, 2)
                        c.wait(u_ready, 1, 1)
                        nc.vector.tensor_tensor(dtu_sb[:], dt_sb[:, q], u_sb[:], ALU.mult
                                                ).then_inc(dtu_ready, 1)
                    if mamba:
                        c.wait(decay_ready, 0, s + 1)
                        c.wait(inject_ready, 0, s + 1)
                        c.wait(state_ready, 0, s - 1)
                        for h in range(2):
                            scan = nc.vector.tensor_tensor_scan(hidden[:, s % 2, h], decay[:, s % 2, h],
                                                                inject[:, h], state[:, h, s:s + 1],
                                                                ALU.mult, ALU.add)
                        scan.then_inc(scan_ready, 1)
                    if ffn and s < 2:
                        t = SLOTS - 2 + s
                        c.wait(hc_ready, -1, t + 1)
                        c.wait(y_step, -1, t)
                        nc.vector.tensor_tensor(y_sum[:], y_sum[:], h_c[:, t % 2], ALU.add).then_inc(y_step, 1)
                    if ffn and s == 1:
                        c.wait(y_step, -1, SLOTS)
                        nc.vector.tensor_tensor(y_gated[:], y_sum[:], z_sb[:, q], ALU.mult).then_inc(y_ready, 1)
                    if mamba:
                        if s == 2:
                            c.wait(hc_ready, 0, 1)
                            c.wait(u_ready, 0, 1)
                            c.wait(y_ready, 0, 0)
                            for h in range(2):
                                step = nc.vector.scalar_tensor_tensor(
                                    out=y_sum[:, h], in0=u_sb[:, h], scalar=vec("D", h), in1=h_c[:, 0, h],
                                    op0=ALU.mult, op1=ALU.add)
                            step.then_inc(y_step, 1)
                        elif s > 2:
                            c.wait(hc_ready, 0, s - 1)
                            c.wait(y_step, 0, s - 2)
                            nc.vector.tensor_tensor(y_sum[:], y_sum[:], h_c[:, s % 2], ALU.add).then_inc(y_step, 1)
                    for d, t in next_state(s, mamba, front):
                        c.wait(dtu_ready, d, 1)
                        c.wait(b_done, d, t + 1)
                        c.wait(scan_ready, d, t)
                        nc.vector.tensor_tensor(inject[:], dtu_sb[:],
                                                over_halves(b_bank(i + d, t)), ALU.mult).then_inc(inject_ready, 1)
                    if experts and s:
                        combine(s - 1)
                    if experts and s == SLOTS - 1:
                        combine(s)
                    if front and s == 7:
                        for k in range(1, TAPS):
                            for h in range(2):
                                if k == 1:
                                    c.wait(conv_first, 1, h + 1)
                                else:
                                    c.wait(conv_step, 1, 2 * (k - 2) + h + 1)
                                nc.vector.scalar_tensor_tensor(
                                    out=u_sb[:, h], in0=conv_in[:, h, k:k + T], scalar=vec("conv_w", TAPS * h + k),
                                    in1=u_sb[:, h], op0=ALU.mult, op1=ALU.add).then_inc(conv_step, 1)

            bodies(dve, body)

        @block.tensor
        def _(pe):
            def product(dst, pairs):
                for n, (stationary, moving) in enumerate(pairs):
                    last = nc.tensor.matmul(dst, stationary, moving, start=(n == 0), stop=(n == len(pairs) - 1))
                return last

            def bias_product():
                pe.wait_ge(weights_in, 16 * 13)
                for k in range(4):
                    last = nc.tensor.matmul(ps_y[:, 0, k:k + 1], win_sb[:, k], vec("ln_b"), start=True, stop=True)
                last.then_inc(start_p, 1)

            def parts_product(dst, w, x_hi, x_lo):
                return product(dst, [(w[0], x_hi), (w[1], x_hi), (w[0], x_lo)])

            def body(i, p, adjacency, front, mamba, ffn, experts):
                c = Count(pe, i)
                q = 1 - p
                for s in range(SLOTS):
                    for d, t in next_state(s, mamba, front):
                        c.wait(lo_ready, d, 1)
                        c.wait(c_ready, d, t)
                        nc.tensor.matmul(ps_c[:, 0], picks(SLOTS + t), bc_parts[:, p if d == 0 else q], start=True,
                                         stop=True).then_inc(c_done, 1)
                    def broadcast_b():
                        for d, t in next_state(s, mamba, front):
                            c.wait(inject_ready, d, max(t - 1, 0) if in_tail(i + d) else t)
                            if in_tail(i) and t == 1 and front:
                                c.wait(agg_ready, 1, 1)
                            nc.tensor.matmul(b_bank(i + d, t), picks(t), bc_parts[:, p if d == 0 else q], start=True,
                                             stop=True).then_inc(b_done, 1)

                    def unit():
                        if s % 2:
                            return
                        u, b = s // 2, s // 4
                        v = 2 * u - 3
                        c.wait(acc_step, -2, 9 * (v // 4) + 2 * (v % 4) + 2 if u >= 2 else 0)
                        if u % 2 == 0:
                            c.wait(lo_split, -2, b + 1)
                        four = slice(4 * (u % 2), 4 * (u % 2) + 4)
                        product(ps_e[:, u % 2], [(H_parts[:, h, split_buffer(p, b), k],
                                                  wd_parts[:, w, k, four].rearrange("p e c -> p (e c)"))
                                                 for k in range(4) for h, w in ((0, 0), (0, 1), (1, 0))]
                                ).then_inc(yexp_done, 1)

                    if not adjacency:
                        broadcast_b()
                        if experts:
                            unit()
                    else:
                        for m in adj_blocks(s):
                            if m == adj_blocks(s)[len(adj_blocks(s)) // 2]:
                                broadcast_b()
                                if experts:
                                    unit()
                            g = m // GROUP
                            if isinstance(i, int) and i == -2 and m == J // 4:
                                bias_product()
                            if m == 0:
                                c.wait(agg_ready, 2, 0)
                            if m % GROUP == 0:
                                fills = GROUPS // RING
                                pe.wait_ge(ring_in[g % RING], c.times_of(16 * fills) + (2 * fills + g // RING + 1) * 16)
                                if isinstance(i, int) and i == -2 and m % (J // 8) == 0:
                                    pe.wait_ge(node_ready, m // (J // 8) + 1)
                            last = nc.tensor.matmul(ps_adj[:, 0], nodes[:, m], ring[:, g % RING, m % GROUP],
                                                    start=(m == 0), stop=(m == J - 1))
                            if m % GROUP == GROUP - 1:
                                last.then_inc(adj_used, 1)
                    if front and s == 0:
                        if isinstance(i, int) and i == -1:
                            pe.wait_ge(start_a, 5)
                            pe.wait_ge(start_v, 11)
                        c.wait(agg_ready, 1, 1)
                        c.wait(dt_ready, 1, 0)
                        product(ps_f[:, 0], [(gcn_sb[:], front_a[:])]).then_inc(gcn_done, 1)
                    if front and s == 1:
                        c.wait(gcn_ready, 1, 1)
                        product(ps_f[:, 0], [(center, front_b[:])]).then_inc(cen_done, 1)
                    if front and s == 2:
                        c.wait(sq_ready, 1, 1)
                        product(ps_f[:, 1], [(mean, front_a[:])]).then_inc(var_done, 1)
                    if ffn and s == 2:
                        c.wait(y_ready, -1, 1)
                        c.wait(base_ready, -1, 0)
                        product(ps_y[:, 0], [(wout_sb[:, h], y_gated[:, h]) for h in range(2)]
                                ).then_inc(wout_done, 1)
                    if ffn and s == 3:
                        c.wait(x1_ready, -1, 1)
                        product(ps_y[:, 0], [(center, x1[:])]).then_inc(cen2_done, 1)
                    if ffn and s == 4:
                        c.wait(sq2_ready, -1, 1)
                        c.wait(cen2_kept, -1, 1)
                        product(ps_y[:, 0], [(mean, ffn_a)]).then_inc(var2_done, 1)
                    if front and s in (5, 6):
                        c.wait(front_lo, 1, 1)
                        for k in range(2):
                            if s == 6:
                                c.wait(xz_ready, 1, k + 1)
                            parts_product(ps_f[:, k], [win_parts[:, h, 2 * (s - 5) + k] for h in range(2)],
                                          norm_hi[:], norm_lo[:]).then_inc(xz_done, 1)
                    if ffn and s == 7:
                        c.wait(ffn_lo, -1, 1)
                        c.wait(xz_ready, 1 if front else 0, 4 if front else 0)
                        for k in range(3):
                            parts_product(h_bank(k), [w1_parts[:, h, k] for h in range(2)], norm_hi[:],
                                          norm_lo[:]).then_inc(h_done, 1)
                    if front and s == 8:
                        c.wait(u_ready, 1, 1)
                        if ffn:
                            c.wait(h_ready, -1, 1)
                        product(ps_f[:, 0], [(wxp_sb[:, h], u_sb[:, h]) for h in range(2)]
                                ).then_inc(dbc_done, 1)
                    if front and s == 9:
                        c.wait(low_split, 1, 1)
                        if ffn:
                            c.wait(h_ready, -1, 2)
                        product(ps_f[:, 1], [(wdt_parts[:, 0], low_parts[0:72])]).then_inc(dt_done, 1)
                    if ffn and s == 9:
                        c.wait(h_ready, -1, 3)
                        parts_product(h_bank(3), [w1_parts[:, h, 3] for h in range(2)], norm_hi[:],
                                      norm_lo[:]).then_inc(h_done, 1)
                    if front and s == 10:
                        c.wait(rest_ready, 1, 1)
                        product(ps_f[:, 0], [(wdt_parts[:, 1], low_parts[0:72])]).then_inc(dt_done, 1)
                    if ffn and s == 10:
                        c.wait(h_ready, -1, 4)
                        for b in range(BLOCKS):
                            last = product(ps_y[:, 0, b * EXPERTS:(b + 1) * EXPERTS],
                                           [(H[:, k, b * P:(b + 1) * P], wg_sb[:, k]) for k in range(4)])
                        last.then_inc(logit_done, 1)
                    if ffn and s == 14:
                        c.wait(gate_step, -1, 12)
                        three = coef_parts[:].bitcast(F32).rearrange("p a b e -> p (a b e)")
                        product(ps_y[0:96, 0, 0:P], [(three, ident)]).then_inc(coef_t_done, 1)
                    if ffn and s == 15:
                        c.wait(coef_t_ready, -1, 1)
                        nc.tensor.matmul(ps_y[:, 0], coef_t, bd_parts[:].rearrange("p b c -> p (b c)"),
                                         start=True, stop=False)
                        for b in range(BLOCKS):
                            last = nc.tensor.matmul(ps_y[:, 0, b * P:(b + 1) * P], x1[:, b * P:(b + 1) * P], ident,
                                                    start=False, stop=(b == BLOCKS - 1))
                        last.then_inc(base_done, 1)

            bodies(pe, body)


def kernel(**inputs):
    import ml_dtypes
    import numpy as np
    import concourse.bacc as bacc
    from concourse.bass_utils import run_bass_kernel_spmd

    a = {k.replace("L0_", ""): np.asarray(v) for k, v in inputs.items()}
    x, adj = a["x"], a["adj"]
    N, D = x.shape
    J = N // P

    def halves(v):
        return v.reshape(2, P, -1).transpose(1, 0, 2)

    vecs = np.zeros((P, NCOLS), np.float32)
    for name, v in (("gcn_b", a["gnn_gcn_b"][:, None]), ("ln_g", a["gnn_ln_g"][:, None]),
                    ("ln_b", a["gnn_ln_b"][:, None]), ("conv_w", halves(a["gnn_conv_w"]).reshape(P, -1)),
                    ("conv_b", a["gnn_conv_b"].reshape(2, P).T), ("b_dt", a["gnn_b_dt"].reshape(2, P).T),
                    ("D", a["gnn_D_skip"].reshape(2, P).T), ("b1", a["ffn_b1"].reshape(4, P).T),
                    ("A_log", halves(a["gnn_A_log"]).reshape(P, -1)),
                    ("bg", np.broadcast_to(a["ffn_bg"], (P, EXPERTS))),
                    ("desc", np.broadcast_to(np.arange(EXPERTS, 0, -1, dtype=np.float32), (P, EXPERTS)))):
        first, n = COLS[name]
        vecs[:, first:first + n] = v
    eye = np.eye(P, dtype=np.float32)
    mean = np.full((P, P), 1.0 / P, np.float32)
    consts = np.stack([eye, eye - mean, mean], axis=1)
    sel = np.tile(np.eye(32), (3, 1)).astype(ml_dtypes.bfloat16)
    w_xp = np.zeros((P, 2, P), np.float32)
    w_dt = np.zeros((72, 2, P), np.float32)
    xp = halves(a["gnn_w_xp"])
    w_xp[:, :, 96:128] = xp[:, :, 8:40]
    for first in (0, 32, 64):
        w_xp[:, :, first:first + 8] = xp[:, :, 0:8]
        w_dt[first:first + 8] = a["gnn_w_dt"].reshape(8, 2, P)
    bd = np.zeros((3, T // P, EXPERTS, T // P, P), np.float32)
    for b in range(T // P):
        bd[:, b, :, b] = a["ffn_bd"]
    bd = bd.reshape(-1, T // P, P)

    arrays = {
        "x_rows": x.reshape(P, J, D), "x_cols": x.T,
        "adj": adj.reshape(N // T, T, P, J // GROUP, GROUP).transpose(0, 3, 2, 4, 1),
        "vecs": vecs, "consts": consts, "sel": sel, "gcn_w": a["gnn_gcn_w"],
        "w_in": a["gnn_w_in"].reshape(P, 4, P), "w_xp": w_xp, "w_dt": w_dt,
        "w_out": halves(a["gnn_w_out"]), "W1": a["ffn_W1"].reshape(P, 4, P),
        "Wg": a["ffn_Wg"].reshape(4, P, EXPERTS).transpose(1, 0, 2),
        "Wd": a["ffn_Wd"].reshape(EXPERTS, 4, P, P).transpose(2, 1, 0, 3), "bd": bd,
    }
    arrays = {k: np.ascontiguousarray(v) for k, v in arrays.items()}
    nc = bacc.Bacc("TRN2", target_bir_lowering=False, num_devices=1)
    args = [nc.dram_tensor(k, v.shape, mybir.dt.from_np(v.dtype), kind="ExternalInput").ap()
            for k, v in arrays.items()]
    out = nc.dram_tensor("out", (N, D), F32, kind="ExternalOutput").ap()
    gnn_mamba_moe(nc, *args, out)
    r = run_bass_kernel_spmd(nc, [arrays], core_ids=[0])
    return r.results[0]["out"]
```
